# Optimizing a Trainium2 kernel written in Bass

```python
import numpy as np
import jax
import jax.numpy as jnp

def _softmax(x, axis=-1):
    return jax.nn.softmax(x, axis=axis)

def _gelu(x):
    return jax.nn.gelu(x, approximate=True)

def _silu(x):
    return jax.nn.silu(x)

def _sigmoid(x):
    return jax.nn.sigmoid(x)

def _layernorm(x, axis=-1, eps=1e-05):
    m = jnp.mean(x, axis=axis, keepdims=True)
    v = jnp.var(x, axis=axis, keepdims=True)
    return (x - m) / jnp.sqrt(v + eps)

def _scatter_add(tgt, idx, src, axis=0):
    return tgt.at[idx].add(src)

def _segment_sum(src, seg, n):
    return jax.ops.segment_sum(src, seg, n)
kernel_name = 'mk_prb_d1_jaxref_r8_9b9305'

def setup_inputs(seed: int=0):
    np.random.seed(seed)
    _w = jnp.asarray

    def _L0_attn_setup():
        import jax, jax.numpy as jnp
        import numpy as np
        ROPE_THETA = 10000.0

        def rope(t, rot_dim):
            S = t.shape[-2]
            half = rot_dim // 2
            inv_freq = 1.0 / ROPE_THETA ** (jnp.arange(0, rot_dim, 2, dtype=jnp.float32) / rot_dim)
            freqs = jnp.arange(S, dtype=jnp.float32)[:, None] * inv_freq[None, :]
            freqs = jnp.repeat(freqs, 2, axis=-1)
            cos, sin = (jnp.cos(freqs), jnp.sin(freqs))
            t_rot, t_pass = (t[..., :rot_dim], t[..., rot_dim:])
            x = t_rot.reshape(*t_rot.shape[:-1], half, 2)
            rh = jnp.stack([-x[..., 1], x[..., 0]], axis=-1).reshape(t_rot.shape)
            t_rot = t_rot * cos + rh * sin
            return jnp.concatenate([t_rot, t_pass], axis=-1)

        def feature_map(x):
            norm = jnp.sqrt(jnp.sum(x * x, axis=-1, keepdims=True))
            return x / jnp.maximum(norm, 1e-12)
        key = jax.random.key(seed)
        kx, kwi, kwo = jax.random.split(key, 3)
        B, S, D = (8, 512, 256)
        scale = 0.02
        return {'X': jax.random.normal(kx, (B, S, D), dtype=jnp.float32), 'W_in': jax.random.normal(kwi, (3 * D, D), dtype=jnp.float32) * scale, 'b_in': jnp.zeros((3 * D,), dtype=jnp.float32), 'W_out': jax.random.normal(kwo, (D, D), dtype=jnp.float32) * scale, 'b_out': jnp.zeros((D,), dtype=jnp.float32)}
    _L0_attn_in = _L0_attn_setup()

    def _L0_ffn_setup():
        import jax, jax.numpy as jnp
        import numpy as np
        E = 64
        K = 6
        CAP = 64
        SCALE = 1.0
        H = 256
        I = 96
        SI = I * 2
        B, S = (2, 128)

        def _moe(x, gate_w, gate_up_proj, down_proj, shared_gate_w, shared_up_w, shared_down_w):
            b, s, h = x.shape
            T = b * s
            xf = x.reshape(T, h)
            scores = jax.nn.softmax(xf @ gate_w.T, axis=-1)
            topk_w, topk_idx = jax.lax.top_k(scores, K)
            topk_w = topk_w * SCALE
            flat_e = topk_idx.reshape(-1)
            order = jnp.argsort(flat_e)
            sorted_e = flat_e[order]
            sorted_tok = (order // K).astype(jnp.int32)
            sorted_w = topk_w.reshape(-1)[order]
            counts = jnp.zeros((E,), jnp.int32).at[flat_e].add(1)
            offsets = jnp.cumsum(counts) - counts
            pos = jnp.arange(T * K, dtype=jnp.int32) - offsets[sorted_e]
            buf_tok = jnp.full((E, CAP), T, jnp.int32).at[sorted_e, pos].set(sorted_tok, mode='drop')
            buf_w = jnp.zeros((E, CAP), x.dtype).at[sorted_e, pos].set(sorted_w, mode='drop')
            xp = jnp.concatenate([xf, jnp.zeros((1, h), x.dtype)], axis=0)
            gx = xp[buf_tok]
            gu = jnp.einsum('ech,ehi->eci', gx, gate_up_proj)
            g, u = jnp.split(gu, 2, axis=-1)
            hid = jax.nn.silu(g) * u
            eo = jnp.einsum('eci,eih->ech', hid, down_proj) * buf_w[..., None]
            routed = jnp.zeros((T + 1, h), x.dtype).at[buf_tok.reshape(-1)].add(eo.reshape(-1, h))[:T]
            shared = jax.nn.silu(xf @ shared_gate_w.T) * (xf @ shared_up_w.T) @ shared_down_w.T
            return (routed + shared).reshape(b, s, h)
        key = jax.random.key(seed)
        ks = jax.random.split(key, 7)
        x = jax.random.normal(ks[0], (B, S, H), jnp.float32)
        gate_w = jax.random.normal(ks[1], (E, H), jnp.float32) * 0.02
        gate_up_proj = jax.random.normal(ks[2], (E, H, 2 * I), jnp.float32) * 0.02
        down_proj = jax.random.normal(ks[3], (E, I, H), jnp.float32) * 0.02
        shared_gate_w = jax.random.normal(ks[4], (SI, H), jnp.float32) * 0.02
        shared_up_w = jax.random.normal(ks[5], (SI, H), jnp.float32) * 0.02
        shared_down_w = jax.random.normal(ks[6], (H, SI), jnp.float32) * 0.02
        return dict(x=x, gate_w=gate_w, gate_up_proj=gate_up_proj, down_proj=down_proj, shared_gate_w=shared_gate_w, shared_up_w=shared_up_w, shared_down_w=shared_down_w)
    _L0_ffn_in = _L0_ffn_setup()
    _d = {'L0_attn_X': _L0_attn_in['X'], 'L0_attn_W_in': _L0_attn_in['W_in'], 'L0_attn_b_in': _L0_attn_in['b_in'], 'L0_attn_W_out': _L0_attn_in['W_out'], 'L0_attn_b_out': _L0_attn_in['b_out'], 'L0_ffn_gate_w': _L0_ffn_in['gate_w'], 'L0_ffn_gate_up_proj': _L0_ffn_in['gate_up_proj'], 'L0_ffn_down_proj': _L0_ffn_in['down_proj'], 'L0_ffn_shared_gate_w': _L0_ffn_in['shared_gate_w'], 'L0_ffn_shared_up_w': _L0_ffn_in['shared_up_w'], 'L0_ffn_shared_down_w': _L0_ffn_in['shared_down_w']}
    _x0 = _d['L0_attn_X']
    _d['L0_attn_X'] = jax.random.normal(jax.random.fold_in(jax.random.key(seed), 1), (2, 1024, 256), dtype=_x0.dtype)
    del _x0
    return _d

def reference(L0_attn_X, L0_attn_W_in, L0_attn_b_in, L0_attn_W_out, L0_attn_b_out, L0_ffn_gate_w, L0_ffn_gate_up_proj, L0_ffn_down_proj, L0_ffn_shared_gate_w, L0_ffn_shared_up_w, L0_ffn_shared_down_w):

    def _L0_attn_ref(X, W_in, b_in, W_out, b_out):
        import jax, jax.numpy as jnp
        import numpy as np
        ROPE_THETA = 10000.0

        def rope(t, rot_dim):
            S = t.shape[-2]
            half = rot_dim // 2
            inv_freq = 1.0 / ROPE_THETA ** (jnp.arange(0, rot_dim, 2, dtype=jnp.float32) / rot_dim)
            freqs = jnp.arange(S, dtype=jnp.float32)[:, None] * inv_freq[None, :]
            freqs = jnp.repeat(freqs, 2, axis=-1)
            cos, sin = (jnp.cos(freqs), jnp.sin(freqs))
            t_rot, t_pass = (t[..., :rot_dim], t[..., rot_dim:])
            x = t_rot.reshape(*t_rot.shape[:-1], half, 2)
            rh = jnp.stack([-x[..., 1], x[..., 0]], axis=-1).reshape(t_rot.shape)
            t_rot = t_rot * cos + rh * sin
            return jnp.concatenate([t_rot, t_pass], axis=-1)

        def feature_map(x):
            norm = jnp.sqrt(jnp.sum(x * x, axis=-1, keepdims=True))
            return x / jnp.maximum(norm, 1e-12)
        D = X.shape[-1]
        QKV = jnp.einsum('bsd,ed->bse', X, W_in) + b_in
        Q, K, V = jnp.split(QKV, 3, axis=-1)
        rot_dim = D // 2
        Q = rope(Q, rot_dim)
        K = rope(K, rot_dim)
        A = jnp.sum(feature_map(K) * V, axis=-2)
        Y = A[:, None, :] * Q
        Y = jnp.einsum('bsd,ed->bse', Y, W_out) + b_out
        return Y + X

    def _L0_ffn_ref(x, gate_w, gate_up_proj, down_proj, shared_gate_w, shared_up_w, shared_down_w):
        import jax, jax.numpy as jnp
        import numpy as np
        E = 64
        K = 6
        CAP = 64
        SCALE = 1.0
        H = 256
        I = 96
        SI = I * 2
        B, S = (2, 128)

        def _moe(x, gate_w, gate_up_proj, down_proj, shared_gate_w, shared_up_w, shared_down_w):
            b, s, h = x.shape
            T = b * s
            xf = x.reshape(T, h)
            scores = jax.nn.softmax(xf @ gate_w.T, axis=-1)
            topk_w, topk_idx = jax.lax.top_k(scores, K)
            topk_w = topk_w * SCALE
            flat_e = topk_idx.reshape(-1)
            order = jnp.argsort(flat_e)
            sorted_e = flat_e[order]
            sorted_tok = (order // K).astype(jnp.int32)
            sorted_w = topk_w.reshape(-1)[order]
            counts = jnp.zeros((E,), jnp.int32).at[flat_e].add(1)
            offsets = jnp.cumsum(counts) - counts
            pos = jnp.arange(T * K, dtype=jnp.int32) - offsets[sorted_e]
            buf_tok = jnp.full((E, CAP), T, jnp.int32).at[sorted_e, pos].set(sorted_tok, mode='drop')
            buf_w = jnp.zeros((E, CAP), x.dtype).at[sorted_e, pos].set(sorted_w, mode='drop')
            xp = jnp.concatenate([xf, jnp.zeros((1, h), x.dtype)], axis=0)
            gx = xp[buf_tok]
            gu = jnp.einsum('ech,ehi->eci', gx, gate_up_proj)
            g, u = jnp.split(gu, 2, axis=-1)
            hid = jax.nn.silu(g) * u
            eo = jnp.einsum('eci,eih->ech', hid, down_proj) * buf_w[..., None]
            routed = jnp.zeros((T + 1, h), x.dtype).at[buf_tok.reshape(-1)].add(eo.reshape(-1, h))[:T]
            shared = jax.nn.silu(xf @ shared_gate_w.T) * (xf @ shared_up_w.T) @ shared_down_w.T
            return (routed + shared).reshape(b, s, h)
        return _moe(x, gate_w, gate_up_proj, down_proj, shared_gate_w, shared_up_w, shared_down_w)
    x = L0_attn_X
    xn = _layernorm(x, axis=-1)
    x = x + _L0_attn_ref(xn, L0_attn_W_in, L0_attn_b_in, L0_attn_W_out, L0_attn_b_out) + _L0_ffn_ref(xn, L0_ffn_gate_w, L0_ffn_gate_up_proj, L0_ffn_down_proj, L0_ffn_shared_gate_w, L0_ffn_shared_up_w, L0_ffn_shared_down_w)
    return x

_drawn_inputs = setup_inputs


def setup_inputs(seed=0):
    import zlib

    import numpy as np

    out = dict(_drawn_inputs(seed))
    spreads = {'L0_attn_b_in': (0.0, 0.423), 'L0_attn_b_out': (0.0, 0.8)}
    factors = {'L0_ffn_gate_w': 8.0,
     'L0_ffn_gate_up_proj': 8.0,
     'L0_ffn_down_proj': 8.0,
     'L0_ffn_shared_gate_w': 7.853,
     'L0_ffn_shared_up_w': 7.729,
     'L0_ffn_shared_down_w': 7.739}
    for name, (base, spread) in spreads.items():
        noise = np.random.default_rng([zlib.crc32(name.encode()), seed]).standard_normal(out[name].shape)
        drawn = base * np.exp(spread * noise) if base else spread * noise
        out[name] = jnp.asarray(drawn.astype(out[name].dtype))
    for name, factor in factors.items():
        out[name] = (out[name] * factor).astype(out[name].dtype)
    return out
```

```python
from contextlib import ExitStack

import concourse.bass as bass
from concourse import mybir

F32 = mybir.dt.float32
F32R = mybir.dt.float32r
U32 = mybir.dt.uint32
I32 = mybir.dt.int32
ALU = mybir.AluOpType
ACT = mybir.ActivationFunctionType
AX_X = mybir.AxisListType.X

P = 128
D = 256
KD = D // P
T = 2048
NT = T // P
NG = 4
TG = NT // NG
GT = TG * P
SEQ_TILES = NT // 2
ROT = D // 2
E = 64
TOPK = 6
CAP = 64
I = 96
SI = 2 * I
NP = E // 2
NW = 3
ROW = D + E
SUMROWS = T + CAP
QKV = 3 * D
SH0 = QKV
WCOLS = SH0 + 2 * SI
EPS = 1e-5
LOWEST = -87.3
PADDED = 1.0
CHOSEN = 2.0
EARLY_T = 12
POOL_T = 5
SLOTS_T = 7
WARM_UP = 44
LAG = 3
PART = 2

B_CHUNK = (0, 1)
B_CHUNK6 = (0, 1, 4, 5, 6, 7)
B_LOGITS = (2, 3)
B_SLOTS = 3
B_GXT = 0
B_H = 1
B_EO = (2, 3)
B_QK = (4, 5)
B_V = 6
B_A = 7
B_SH = (4, 5, 6)
B_SHD = 7
B_QT = (4, 5)
B_OUT = (6, 7)

FILL = [[] for _ in range(NP)]
for _t in range(EARLY_T, NT):
    FILL[_t - EARLY_T] += [("qkv", _t)]
_at = NT - EARLY_T
FILL[_at + 1] += [("scale", 0)]
FILL[_at + 5] += [("scale", 1)]
for _g in range(NG):
    for _b in range(3):
        FILL[_at + 4 * _g + _b] += [("up", _g, _b)]
    FILL[_at + 4 * _g + 3] += [("hid", _g)]
    FILL[_at + 4 * _g + 4] += [("split", _g)]
    _i = _at + 4 * _g + (6 if _g < NG - 1 else 5)
    FILL[_i] += [("down", 2 * _g)]
    FILL[_i + 1] += [("down", 2 * _g + 1)]
_at += 4 * NG + 2
for _t in range(NT):
    FILL[_t] += [("rotq", _t)]
    FILL[_at + _t * (NP - _at) // NT] += [("qt", _t)]


def build(nc, X, W_in, b_in, W_out, b_out, gate_w, gate_up, down, sh_gate, sh_up, sh_down,
          cos_t, sin_t, out, rows, sums):
    x_d = X.rearrange("b s d -> (b s) d").rearrange("(n p) d -> p n d", p=P)
    out_d = out.rearrange("b s d -> (b s) d").rearrange("(n p) d -> p n d", p=P)
    rows_d = rows.rearrange("(n p) c -> p n c", p=P)

    order = [("norm", 0), ("gate", 0), ("x", 0), ("x", 1), ("norm", 1), ("x", 2), ("x", 3), ("logits", 0)]
    order += [("norm", 2), ("x", 4), ("x", 5), ("logits", 1), ("x", 6), ("x", 7), ("exp", 0), ("logits", 2)]
    order += [("w", 0), ("logits", 3), ("exp", 1), ("w", 1), ("w", 2), ("exp", 2), ("bias", 0), ("w", 3), ("exp", 3)]
    order += [("w", 4), ("key", 0), ("key", 1), ("qkv", 0), ("qkv", 1), ("sd", 0), ("wo", 0)]
    order += [("qkv", t) for t in range(2, SLOTS_T)] + [("slots", 0)] + [("qkv", t) for t in range(SLOTS_T, EARLY_T)]
    chunks = [c for c in order if c[0] in ("gate", "x", "w", "key", "sd", "wo")]
    number = {c: n for n, c in enumerate(chunks)}
    before_qkv = [c for c in order[:order.index(("qkv", 0))] if c in number]
    bank_of = {c: B_CHUNK6[n % 6] if c in before_qkv else B_CHUNK[n % 2] for n, c in enumerate(chunks)}
    freed = {c: max([m + 1 for m, d in enumerate(chunks[:n]) if bank_of[d] == bank_of[c]], default=0)
             for n, c in enumerate(chunks)}

    def lows(n):
        return sum(c[0] in ("gate", "x") for c in chunks[:n])

    with ExitStack() as ctx:
        def sb(name, shape, dt=F32):
            return ctx.enter_context(nc.sbuf_tensor(name, shape, dt))

        def sem(name):
            return ctx.enter_context(nc.semaphore(name))

        x = sb("x", [P, NT, D])
        scores = sb("scores", [P, NT, E])
        w_stage = sb("w_stage", [P, 2, 4 * P])
        xT_hi = sb("xT_hi", [P, KD, T], F32R)
        xT_lo = sb("xT_lo", [P, KD, T], F32R)
        w_raw = sb("w_raw", [P, 12, D])
        sd_raw = sb("sd_raw", [P, KD, SI])
        wT_hi = sb("wT_hi", [P, KD, WCOLS], F32R)
        wT_lo = sb("wT_lo", [P, KD, WCOLS], F32R)
        gateT = sb("gateT", [P, KD, 2 * E], F32R)
        lg = sb("lg", [P, 2, TG, E])
        woT = sb("woT", [P, KD, D])
        woA = sb("woA", [P, 2, KD, D])
        woA_hi = sb("woA_hi", [P, 2, KD, D], F32R)
        woA_lo = sb("woA_lo", [P, 2, KD, D], F32R)
        sdT_hi = sb("sdT_hi", [P, 2, D], F32R)
        sdT_lo = sb("sdT_lo", [P, 2, D], F32R)
        ident = sb("ident", [P, P])
        ones = sb("ones", [P, P], F32R)
        bias_hl = sb("bias_hl", [P, QKV + D], F32R)
        cos = sb("cos", [P, SEQ_TILES, ROT])
        sin = sb("sin", [P, SEQ_TILES, ROT])
        stats = sb("stats", [P, NT, 6])
        mv = sb("mv", [P, NT, 2])
        var = sb("var", [P, NT])
        rstd = sb("rstd", [P, NT])
        nmr = sb("nmr", [P, NT])
        minus_half = sb("minus_half", [P, TG])
        kconst_i = sb("kconst_i", [P, NT], I32)
        kconst = sb("kconst", [P, NT])
        cpart_i = sb("cpart_i", [P, 1], I32)
        cpart = sb("cpart", [P, 1])
        base = sb("base", [P, 1])
        best = sb("best", [P, NT, 8])
        best_sh = sb("best_sh", [P, TG, 8])
        shifted = sb("shifted", [P, 2, TG, E + 2])
        marked = sb("marked", [P, TG, E + 2])
        expo = sb("expo", [P, 2, TG, E])
        esum = sb("esum", [P, NT])
        einv = sb("einv", [P, NT])
        cand = sb("cand", [P, CAP])
        other = sb("other", [E, CAP])
        slots = sb("slots", [E, 2, CAP])
        keyc = sb("keyc", [P, NP])
        tokf = sb("tokf", [P, NP])
        padc = sb("padc", [P, NP])
        from_row = sb("from_row", [P, NP], U32)
        to_row = sb("to_row", [P, NP], U32)
        q = sb("q", [P, NT, D])
        k = sb("k", [P, 3, D])
        v = sb("v", [P, 3, D])
        ksq = sb("ksq", [P, D])
        rot_q = sb("rot_q", [P, 2, ROT])
        rot_k = sb("rot_k", [P, 2, ROT])
        kv = sb("kv", [P, 3, D])
        ss = sb("ss", [P, NT])
        ssm = sb("ssm", [P, NT])
        rnorm = sb("rnorm", [P, NT])
        acol = sb("acol", [P, 4])
        sh_sg = sb("sh_sg", [P, 2, GT])
        sh_hid = sb("sh_hid", [P, 2, GT])
        sh_hi = sb("sh_hi", [P, 2, GT], F32R)
        sh_lo = sb("sh_lo", [P, 2, GT], F32R)
        qT_hi = sb("qT_hi", [P, 2, KD, P], F32R)
        qT_lo = sb("qT_lo", [P, 2, KD, P], F32R)
        gu = sb("gu", [P, NW, 2, KD, 2 * I])
        dn = sb("dn", [I, NW, 2, D])
        gx = sb("gx", [P, 4, ROW])
        gxT = sb("gxT", [P, 2, KD, P])
        sg = sb("sg", [P, I])
        hid = sb("hid", [P, I])
        hidT = sb("hidT", [I, P])
        wsl = sb("wsl", [P, 4])
        eo = sb("eo", [P, 4, D])
        zeros = sb("zeros", [P, D])
        xn = q
        bias = sh_hid[:, :, :].rearrange("p a n -> p (a n)")
        bias_top = sh_sg[:, :, :].rearrange("p a n -> p (a n)")
        key = woA[:, :, :, :].rearrange("p s k d -> p (s k d)").rearrange("p (j h e) -> p j h e", h=2, e=E)
        keyT = eo[:, :, :].rearrange("p r d -> p (r d)")

        ps = ctx.enter_context(nc.psum_tensor("ps", [P, 8, 512], F32))

        x_in = [sem(f"x_in{g}") for g in range(NG)]
        gate_in = sem("gate_in")
        win_in = sem("win_in")
        wout_in = sem("wout_in")
        sh_in = sem("sh_in")
        sd_in = sem("sd_in")
        table_in = sem("table_in")
        bias_in = sem("bias_in")
        ident_ok = sem("ident_ok")
        iota_ok = sem("iota_ok")
        vconst_ok = sem("vconst_ok")
        vstep = sem("vstep")
        gstep = sem("gstep")
        var_ok = sem("var_ok")
        rstd_ok = sem("rstd_ok")
        nmr_ok = sem("nmr_ok")
        xn_ok = sem("xn_ok")
        resid_ok = sem("resid_ok")
        chunk_ok = sem("chunk_ok")
        hi_ok = sem("hi_ok")
        lo_ok = sem("lo_ok")
        wlo_ok = sem("wlo_ok")
        logits_ok = sem("logits_ok")
        lg_ok = sem("lg_ok")
        shifted_ok = sem("shifted_ok")
        exp_ok = sem("exp_ok")
        einv_ok = sem("einv_ok")
        marked_ok = sem("marked_ok")
        scores_ok = sem("scores_ok")
        xn_out = [sem(f"xn_out{g}") for g in range(NG)]
        scores_out = sem("scores_out")
        zero_out = sem("zero_out")
        bias_hi_ok = sem("bias_hi_ok")
        bias_ok = sem("bias_ok")
        qkv_ok = sem("qkv_ok")
        qkv_copied = sem("qkv_copied")
        v_copied = sem("v_copied")
        qrot_ok = sem("qrot_ok")
        kv_ok = sem("kv_ok")
        rnorm_ok = sem("rnorm_ok")
        a_ok = sem("a_ok")
        acol_ok = sem("acol_ok")
        woa_ok = sem("woa_ok")
        slots_ok = sem("slots_ok")
        slotsT_ok = sem("slotsT_ok")
        index_ok = sem("index_ok")
        shup_ok = sem("shup_ok")
        silu_ok = sem("silu_ok")
        shid_ok = sem("shid_ok")
        shhi_ok = sem("shhi_ok")
        shlo_ok = sem("shlo_ok")
        shd_ok = sem("shd_ok")
        shadd_ok = sem("shadd_ok")
        qt_ok = sem("qt_ok")
        qhi_ok = sem("qhi_ok")
        qlo_ok = sem("qlo_ok")
        dense_ok = sem("dense_ok")
        dadd_ok = sem("dadd_ok")
        gu_in = [sem(f"gu_in{r}") for r in range(NW)]
        dn_in = [sem(f"dn_in{r}") for r in range(NW)]
        gx_in = [sem(f"gx_in{r}") for r in range(4)]
        gtr_ok = sem("gtr_ok")
        gxT_ok = sem("gxT_ok")
        up_ok = sem("up_ok")
        sg_ok = sem("sg_ok")
        hid_ok = sem("hid_ok")
        ht_ok = sem("ht_ok")
        hidT_ok = sem("hidT_ok")
        wsl_ok = sem("wsl_ok")
        down_ok = sem("down_ok")
        eo_ok = sem("eo_ok")
        scattered = sem("scattered")
        sum_in = [sem(f"sum_in{g}") for g in range(NT // PART)]
        half_sum = sem("half_sum")
        total_ok = sem("total_ok")
        out_done = sem("out_done")

        block = ctx.enter_context(nc.Block())

        def tiles(g):
            return range(TG * g, TG * g + TG)

        def logits(t):
            j = t % TG
            return ps[:, B_LOGITS[t // TG % 2], 2 * E * j:2 * E * j + 2 * E]

        def w_cols(n):
            return slice(2 * P * n, min(2 * P * n + 2 * P, WCOLS))

        def rotate(eng, done, a, tmp, c, s):
            pairs = a[:, 0:ROT].rearrange("p (h two) -> p h two", two=2)
            done(eng.tensor_tensor(tmp[:, 0, :], a[:, 0:ROT], c, ALU.mult))
            done(eng.tensor_tensor(tmp[:, 1, :].rearrange("p (h two) -> p h two", two=2), pairs[:, :, ::-1],
                                   s.rearrange("p (h two) -> p h two", two=2), ALU.mult))
            return eng.tensor_tensor(a[:, 0:ROT], tmp[:, 0, :], tmp[:, 1, :], ALU.add)

        def tables(t):
            return cos[:, t % SEQ_TILES, :], sin[:, t % SEQ_TILES, :]

        def rotate_k(eng, done, t):
            eng.wait_ge(qkv_copied, t + 1)
            done(rotate(eng, done, k[:, t % 3, :], rot_k, *tables(t)))
            if t >= 3:
                eng.wait_ge(a_ok, t - 2)
            eng.tensor_tensor(kv[:, t % 3, :], k[:, t % 3, :], v[:, t % 3, :], ALU.mult).then_inc(kv_ok, 1)

        @block.sync
        def _(sp):
            sp.dma_start(w_raw[0:E, 11, :], gate_w).then_inc(gate_in, 16)
            for g in range(NG):
                sp.dma_start(x[:, TG * g:TG * g + TG, :], x_d[:, TG * g:TG * g + TG, :]).then_inc(x_in[g], 16)
            sp.dma_start(w_raw[:, 0:6, :], W_in.rearrange("(n p) d -> p n d", p=P)).then_inc(win_in, 16)
            for b, n in ((b_in, 0), (b_out, QKV)):
                for r in (0, 32):
                    sp.dma_start(bias[r:r + 1, n:n + b.shape[0]], b.rearrange("(a n) -> a n", a=1)).then_inc(bias_in, 16)

            def weights(i):
                if i >= NW:
                    sp.wait_ge(up_ok, i - NW + 1)
                sp.dma_start(gu[:, i % NW, :, :, :],
                             gate_up[2 * i:2 * i + 2].rearrange("e (p k) n -> p e k n", k=KD)).then_inc(gu_in[i % NW], 16)
                if i >= NW:
                    sp.wait_ge(down_ok, i - NW + 1)
                sp.dma_start(dn[:, i % NW, :, :], down[2 * i:2 * i + 2].rearrange("e i d -> i e d")).then_inc(dn_in[i % NW], 16)

            sums_p = sums.rearrange("(p n) d -> p n d", p=P)
            share = 2 * SUMROWS // P // 3
            for g in range(NG):
                sp.wait_ge(xn_ok, TG * g + TG)
                sp.dma_start(rows_d[:, TG * g:TG * g + TG, 0:D], xn[:, TG * g:TG * g + TG, :]).then_inc(xn_out[g], 16)
                if g == 0:
                    sp.dma_start(cos[:, :, :], cos_t.rearrange("(n p) d -> p n d", p=P)).then_inc(table_in, 16)
                    sp.dma_start(sin[:, :, :], sin_t.rearrange("(n p) d -> p n d", p=P)).then_inc(table_in, 16)
                elif g == 1:
                    sp.dma_start(w_raw[:, 8, :], sh_gate[0:P, :]).then_inc(sh_in, 16)
                    sp.dma_start(w_raw[0:SI - P, 9, :], sh_gate[P:SI, :]).then_inc(sh_in, 16)
                    sp.dma_start(w_raw[SI - P:P, 9, :], sh_up[P:SI, :]).then_inc(sh_in, 16)
                    sp.dma_start(w_raw[:, 10, :], sh_up[0:P, :]).then_inc(sh_in, 16)
                elif g == 2:
                    sp.dma_start(sd_raw[:, :, :], sh_down.rearrange("(n p) i -> p n i", p=P)).then_inc(sd_in, 16)
                    sp.dma_start(w_raw[:, 6:8, :], W_out.rearrange("(n p) d -> p n d", p=P)).then_inc(wout_in, 16)
            for n in range(NG):
                sp.wait_ge(scores_ok, n + 1)
                sp.dma_start(rows_d[:, TG * n:TG * n + TG, D:ROW], scores[:, TG * n:TG * n + TG, :]).then_inc(scores_out, 16)
            weights(0)
            weights(1)
            weights(2)
            sp.wait_ge(vconst_ok, 1)
            for n in range(3):
                sp.dma_start(sums_p[:, share * n:share * n + share, :],
                             zeros[:, None, :].to_broadcast([P, share, D])).then_inc(zero_out, 16)
            for i in range(NW, NP):
                weights(i)
            sp.wait_ge(scattered, 16 * NP)
            sp.wait_ge(qt_ok, NT)
            sums_d = sums.rearrange("(s r) d -> s r d", s=2)
            for n in range(NT // PART):
                part = slice(PART * P * n, PART * P * n + PART * P)
                sp.dma_start(q[:, PART * n:PART * n + PART, :],
                             sums_d[0, part, :].rearrange("(n p) d -> p n d", p=P)).then_inc(sum_in[n], 16)
                if n >= 4:
                    sp.wait_ge(total_ok, n - 3)
                sp.dma_start(w_raw[:, PART * (n % 4):PART * (n % 4) + PART, :],
                             sums_d[1, part, :].rearrange("(n p) d -> p n d", p=P)).then_inc(sum_in[n], 16)
            sp.wait_ge(out_done, 16 * NT // PART)

        @block.gpsimd
        def _(pool):
            steps = [0]

            def done(ins):
                steps[0] += 1
                ins.then_inc(gstep, 1)
                pool.wait_ge(gstep, steps[0])

            done(pool.memset(ident[:, :], 0.0))
            pool.affine_select(out=ident[:, :], in_=ident[:, :], compare_op=ALU.not_equal, fill=1.0, base=0,
                               pattern=[[-1, P]], channel_multiplier=1).then_inc(ident_ok, 1)
            pool.wait_ge(ident_ok, 1)
            done(pool.memset(minus_half[:, :], -0.5))
            done(pool.memset(base[0:P // 2, :], float(T)))
            done(pool.memset(base[P // 2:P, :], float(T + SUMROWS)))
            done(pool.iota(kconst_i[:, :], pattern=[[-P, NT]], base=T, channel_multiplier=-1))
            done(pool.iota(cpart_i[0:P // 2, :], pattern=[[0, 1]], base=0, channel_multiplier=1))
            pool.iota(cpart_i[P // 2:P, :], pattern=[[0, 1]], base=0, channel_multiplier=1).then_inc(iota_ok, 1)
            pool.wait_ge(iota_ok, 1)

            def rstds(g):
                pool.wait_ge(var_ok, g + 1)
                s = slice(TG * g, TG * g + TG)
                pool.tensor_tensor(rstd[:, s], var[:, s], minus_half[:, :], ALU.pow).then_inc(rstd_ok, 1)

            def residual(g):
                pool.wait_ge(xn_ok, TG * g + TG)
                s = slice(TG * g, TG * g + TG)
                pool.tensor_tensor(x[:, s, :], x[:, s, :], xn[:, s, :], ALU.add).then_inc(resid_ok, 1)

            def group_scores(g):
                pool.wait_ge(exp_ok, TG * g + TG)
                pool.wait_ge(einv_ok, g + 1)
                s = slice(TG * g, TG * g + TG)
                pool.tensor_tensor(scores[:, s, :], expo[:, g % 2, :, :],
                                   einv[:, s].unsqueeze(2).to_broadcast([P, TG, E]), ALU.mult).then_inc(scores_ok, 1)

            def weight_low(n, c):
                pool.wait_ge(hi_ok, number[c] + 1)
                stage = w_stage[:, n % 2, :]
                if c[0] == "w":
                    cols = w_cols(c[1])
                    m = cols.stop - cols.start
                    pool.tensor_tensor(wT_lo[:, :, cols], stage[:, 0:KD * m].rearrange("p (k m) -> p k m", k=KD),
                                       wT_hi[:, :, cols].bitcast(F32), ALU.subtract).then_inc(wlo_ok, 1)
                else:
                    st = stage.rearrange("p (k m) -> p k m", k=2)
                    done(pool.tensor_tensor(sdT_lo[:, 0, :], st[:, 0, :], sdT_hi[:, 0, :].bitcast(F32), ALU.subtract))
                    pool.tensor_tensor(sdT_lo[0:SI - P, 1, :], st[0:SI - P, 1, :],
                                       sdT_hi[0:SI - P, 1, :].bitcast(F32), ALU.subtract).then_inc(wlo_ok, 1)

            def inverse_norm(t):
                pool.wait_ge(qkv_copied, t + 1)
                done(pool.tensor_scalar(ssm[:, t:t + 1], ss[:, t:t + 1], 1e-24, None, ALU.max))
                pool.tensor_tensor(rnorm[:, t:t + 1], ssm[:, t:t + 1], minus_half[:, 0:1], ALU.pow).then_inc(rnorm_ok, 1)

            n_low = 0
            for g in range(NG):
                rstds(g)
            for c in order:
                if c[0] == "x" and c[1] % 2:
                    residual(c[1] // 2)
                elif c[0] == "exp":
                    group_scores(c[1])
                elif c[0] in ("w", "sd"):
                    weight_low(n_low, c)
                    n_low += 1
                elif c[0] == "bias":
                    pool.wait_ge(wlo_ok, n_low)
                    pool.wait_ge(scores_ok, 3)
                    pool.wait_ge(bias_hi_ok, 2)
                    pool.tensor_tensor(bias_hl[32:33, :], bias[32:33, :], bias_top[32:33, :],
                                       ALU.subtract).then_inc(bias_ok, 1)
                    pool.wait_ge(bias_ok, 1)
                elif c[0] == "qkv":
                    if c[1] == 0:
                        pool.wait_ge(table_in, 32)
                    if c[1] < POOL_T:
                        inverse_norm(c[1])
                        rotate_k(pool, done, c[1])

            def gather(i):
                if i >= 4:
                    pool.wait_ge(gtr_ok, i - 3)
                    pool.wait_ge(wsl_ok, 2 * (i - 3))
                pool.indirect_dma_start(gx[:, i % 4, :], None, rows[:, :],
                                        bass.IndirectOffsetOnAxis(ap=from_row[:, i:i + 1], axis=0),
                                        bounds_check=T - 1, oob_is_err=False).then_inc(gx_in[i % 4], 16)

            pool.wait_ge(index_ok, 1)
            for g in range(NG):
                pool.wait_ge(xn_out[g], 16)
            pool.wait_ge(scores_out, 16 * NG)
            for i in range(4):
                gather(i)
            for t in range(POOL_T, EARLY_T):
                inverse_norm(t)
            gather(4)
            gather(5)
            pool.wait_ge(zero_out, 48)
            for i in range(NP):
                if i + 6 < NP:
                    gather(i + 6)
                for f in FILL[i - 1] if i else []:
                    if f[0] == "qkv":
                        inverse_norm(f[1])
                pool.wait_ge(eo_ok, i + 1)
                if i:
                    pool.wait_ge(scattered, 16 * i)
                pool.indirect_dma_start(sums[:, :], bass.IndirectOffsetOnAxis(ap=to_row[:, i:i + 1], axis=0),
                                        eo[:, i % 4, :], None, bounds_check=2 * SUMROWS - 1, oob_is_err=True,
                                        compute_op=ALU.add).then_inc(scattered, 16)
            pool.wait_ge(scattered, 16 * NP)

        @block.scalar
        def _(act):
            def qkv_copy(t):
                act.wait_ge(qkv_ok, t + 1)
                bank = ps[:, B_QK[t % 2], :]
                act.wait_ge(xn_out[t // TG], 16)
                act.wait_ge(resid_ok, t // TG + 1)
                act.activation(q[:, t, :], bank[:, 0:D], ACT.Copy)
                if t >= 3:
                    act.wait_ge(kv_ok, t - 2)
                act.activation(k[:, t % 3, :], bank[:, D:2 * D], ACT.Copy)
                act.activation(v[:, t % 3, :], ps[:, B_V, 0:D], ACT.Copy).then_inc(v_copied, 1)
                if t:
                    act.wait_ge(qkv_copied, t)
                act.activation(ksq[:, :], bank[:, D:2 * D], ACT.Square,
                               accum_out=ss[:, t:t + 1]).then_inc(qkv_copied, 1)

            n_low = 0
            for c in order:
                if c[0] in ("gate", "x", "w", "key", "sd", "wo"):
                    n = number[c]
                    bank = ps[:, bank_of[c], :]
                    act.wait_ge(chunk_ok, n + 1)
                if c[0] == "norm":
                    act.wait_ge(nmr_ok, c[1] + 1)
                    for t in tiles(c[1]):
                        act.activation(xn[:, t, :], x[:, t, :], ACT.Identity, bias=nmr[:, t:t + 1],
                                       scale=rstd[:, t:t + 1]).then_inc(xn_ok, 1)
                elif c[0] == "gate":
                    act.activation(gateT[:, :, 0:E], bank[:, 0:KD * E].rearrange("p (k e) -> p k e", k=KD),
                                   ACT.Copy).then_inc(hi_ok, 1)
                elif c[0] == "x":
                    g, kd = c[1] // 2, c[1] % 2
                    act.activation(xT_hi[:, kd, GT * g:GT * g + GT], bank, ACT.Copy).then_inc(hi_ok, 1)
                elif c[0] == "w":
                    cols = w_cols(c[1])
                    m = cols.stop - cols.start
                    if n_low >= 2:
                        act.wait_ge(wlo_ok, n_low - 1)
                    act.activation(w_stage[:, n_low % 2, 0:KD * m], bank[:, 0:KD * m], ACT.Copy)
                    act.activation(wT_hi[:, :, cols], bank[:, 0:KD * m].rearrange("p (k m) -> p k m", k=KD),
                                   ACT.Copy).then_inc(hi_ok, 1)
                    n_low += 1
                elif c[0] == "bias":
                    act.wait_ge(bias_in, 64)
                    act.wait_ge(vconst_ok, 2)
                    act.activation(bias_hl[0:1, :], bias[0:1, :], ACT.Copy).then_inc(bias_hi_ok, 1)
                    act.activation(bias_top[32:33, :].bitcast(F32R), bias[32:33, :], ACT.Copy).then_inc(bias_hi_ok, 1)
                elif c[0] == "sd":
                    act.wait_ge(wlo_ok, n_low - 1)
                    b2 = bank.rearrange("p (k m) -> p k m", k=2)
                    st = w_stage[:, n_low % 2, :].rearrange("p (k m) -> p k m", k=2)
                    act.activation(st[:, 0, :], b2[:, 0, :], ACT.Copy)
                    act.activation(st[0:SI - P, 1, :], b2[0:SI - P, 1, :], ACT.Copy)
                    act.activation(sdT_hi[:, 0, :], b2[:, 0, :], ACT.Copy)
                    act.activation(sdT_hi[0:SI - P, 1, :], b2[0:SI - P, 1, :], ACT.Copy).then_inc(hi_ok, 1)
                    n_low += 1
                elif c[0] == "wo":
                    act.activation(woT[:, :, :], bank.rearrange("p (k m) -> p k m", k=KD), ACT.Copy).then_inc(hi_ok, 1)
                elif c[0] == "key":
                    act.activation(keyT[:, 4 * P * c[1]:4 * P * c[1] + 4 * P], bank, ACT.Copy).then_inc(hi_ok, 1)
                elif c[0] == "exp":
                    g = c[1]
                    if g >= 2:
                        act.wait_ge(scores_ok, g - 1)
                    for j in range(TG):
                        t = TG * g + j
                        act.wait_ge(shifted_ok, t + 1)
                        act.activation(expo[:, g % 2, j, :], shifted[:, g % 2, j, 0:E], ACT.Exp,
                                       accum_out=esum[:, t:t + 1]).then_inc(exp_ok, 1)
                elif c[0] == "qkv":
                    qkv_copy(c[1])

            def gxT_copy(i):
                act.wait_ge(gtr_ok, i + 1)
                if i >= 2:
                    act.wait_ge(up_ok, i - 1)
                act.activation(gxT[:, i % 2, :, :], ps[:, B_GXT, 0:D].rearrange("p (k c) -> p k c", k=KD),
                               ACT.Copy).then_inc(gxT_ok, 1)

            def silu(i):
                act.wait_ge(up_ok, i + 1)
                if i:
                    act.wait_ge(hid_ok, i)
                act.activation(sg[:, :], ps[:, B_H, 0:I], ACT.Silu).then_inc(sg_ok, 1)

            gxT_copy(0)
            silu(0)
            gxT_copy(1)
            for i in range(NP):
                act.wait_ge(ht_ok, i + 1)
                if i + 2 < NP:
                    gxT_copy(i + 2)
                if i:
                    act.wait_ge(down_ok, i)
                act.activation(hidT[:, :], ps[0:I, B_GXT, D:D + P], ACT.Copy).then_inc(hidT_ok, 1)
                if i + 1 < NP:
                    silu(i + 1)
                for f in FILL[i]:
                    if f[0] == "qkv":
                        qkv_copy(f[1])
                    elif f[0] == "hid":
                        g = f[1]
                        act.wait_ge(shup_ok, 3 * g + 3)
                        if g:
                            act.wait_ge(shid_ok, 2 * g)
                        act.activation(sh_sg[:, 0, :], ps[:, B_SH[0], :], ACT.Silu).then_inc(silu_ok, 1)
                        act.activation(sh_sg[0:SI - P, 1, :], ps[0:SI - P, B_SH[1], :], ACT.Silu).then_inc(silu_ok, 1)
                    elif f[0] == "split":
                        g = f[1]
                        act.wait_ge(shid_ok, 2 * g + 1)
                        if g:
                            act.wait_ge(shd_ok, 2 * g)
                        act.activation(sh_hi[:, 0, :], sh_hid[:, 0, :], ACT.Copy).then_inc(shhi_ok, 1)
                        act.wait_ge(shid_ok, 2 * g + 2)
                        act.activation(sh_hi[0:SI - P, 1, :], sh_hid[0:SI - P, 1, :], ACT.Copy).then_inc(shhi_ok, 1)
                    elif f[0] == "qt":
                        t = f[1]
                        act.wait_ge(qt_ok, t + 1)
                        if t >= 2:
                            act.wait_ge(dense_ok, t - 1)
                        act.activation(qT_hi[:, t % 2, :, :], ps[:, B_QT[t % 2], 0:D].rearrange("p (k c) -> p k c", k=KD),
                                       ACT.Copy).then_inc(qhi_ok, 1)
            for n in range(NT // PART):
                act.wait_ge(total_ok, n + 1)
                act.dma_start(out_d[:, PART * n:PART * n + PART, :], x[:, PART * n:PART * n + PART, :]).then_inc(out_done, 16)
            act.wait_ge(out_done, 16 * NT // PART)

        def passes(hi_a, lo_a, hi_b, lo_b):
            return ((hi_a, hi_b), (hi_a, lo_b), (lo_a, hi_b))

        @block.tensor
        def _(pe):
            def a_sum(t):
                pe.wait_ge(kv_ok, t + 1)
                pe.wait_ge(rnorm_ok, t + 1)
                for h in range(KD):
                    mm = pe.matmul(ps[:, B_A, 2 * (t // SEQ_TILES) + h:2 * (t // SEQ_TILES) + h + 1],
                                   kv[:, t % 3, P * h:P * h + P], rnorm[:, t:t + 1],
                                   start=(t == 0 and h == 0), stop=(t == NT - 1), skip_group_check=True)
                mm.then_inc(a_ok, 1)

            def project(t):
                if t == 0:
                    pe.wait_ge(wlo_ok, 3)
                    pe.wait_ge(hi_ok, number[("w", 2)] + 1)
                    pe.wait_ge(bias_ok, 1)
                if t < 2:
                    n = max(number[c] for c in before_qkv if bank_of[c] in (B_QK[t], B_V, B_A))
                    pe.wait_ge(hi_ok, n + 1)
                    pe.wait_ge(lo_ok, lows(n + 1))
                else:
                    pe.wait_ge(qkv_copied, t - 1)
                for o, cols in ((ps[:, B_QK[t % 2], :], slice(0, 2 * D)), (ps[:, B_V, 0:D], slice(2 * D, 3 * D))):
                    if t and cols.start:
                        pe.wait_ge(v_copied, t)
                    mms = [(ones[:, :], bias_hl[:, cols])]
                    mms += [(a[:, kd, P * t:P * t + P], b[:, kd, cols])
                            for kd in range(KD) for a, b in passes(xT_hi, xT_lo, wT_hi, wT_lo)]
                    for m, (a, b) in enumerate(mms):
                        mm = pe.matmul(o, a, b, start=(m == 0), stop=(m == len(mms) - 1))
                mm.then_inc(qkv_ok, 1)
                if t >= LAG:
                    a_sum(t - LAG)

            pe.wait_ge(ident_ok, 1)
            for _ in range(WARM_UP):
                pe.transpose(ps[:, B_A, 0:P], ident[:, :], ident[:, :])
            pe.wait_ge(gate_in, 16)
            for c in order:
                if c[0] in ("gate", "x", "w", "key", "sd", "wo"):
                    n = number[c]
                    bank = ps[:, bank_of[c], :]
                    if freed[c]:
                        pe.wait_ge(hi_ok, freed[c])
                        pe.wait_ge(lo_ok, lows(freed[c]))
                if c[0] == "gate":
                    for kd in range(KD):
                        tr = pe.transpose(bank[:, E * kd:E * kd + E], w_raw[0:E, 11, P * kd:P * kd + P], ident[0:E, 0:E])
                    tr.then_inc(chunk_ok, 1)
                elif c[0] == "x":
                    g, kd = c[1] // 2, c[1] % 2
                    for j, t in enumerate(tiles(g)):
                        pe.wait_ge(xn_ok, t + 1)
                        tr = pe.transpose(bank[:, P * j:P * j + P], xn[:, t, P * kd:P * kd + P], ident[:, :])
                    tr.then_inc(chunk_ok, 1)
                elif c[0] == "w":
                    pe.wait_ge(*((win_in, 16) if c[1] < 3 else (sh_in, 64)))
                    blocks = (w_cols(c[1]).stop - w_cols(c[1]).start) // P
                    for b in range(blocks):
                        for kd in range(KD):
                            src = 2 * c[1] + b if c[1] < 3 else 2 * c[1] + b + 2
                            at = P * (blocks * kd + b)
                            tr = pe.transpose(bank[:, at:at + P], w_raw[:, src, P * kd:P * kd + P], ident[:, :])
                    tr.then_inc(chunk_ok, 1)
                elif c[0] == "sd":
                    pe.wait_ge(sd_in, 16)
                    for b in range(2):
                        pe.transpose(bank[:, P * b:P * b + P], sd_raw[:, b, 0:P], ident[:, :])
                        tr = pe.transpose(bank[0:SI - P, D + P * b:D + P * b + P], sd_raw[:, b, P:SI], ident[:, :])
                    tr.then_inc(chunk_ok, 1)
                elif c[0] == "wo":
                    pe.wait_ge(wout_in, 16)
                    for kd in range(KD):
                        for b in range(2):
                            at = P * (2 * kd + b)
                            tr = pe.transpose(bank[:, at:at + P], w_raw[:, 6 + b, P * kd:P * kd + P], ident[:, :])
                    tr.then_inc(chunk_ok, 1)
                elif c[0] == "key":
                    pe.wait_ge(marked_ok, NG)
                    for j in range(4):
                        tr = pe.transpose(bank[:, P * j:P * j + P],
                                          key[:, 4 * c[1] + j, :, :].rearrange("p h e -> p (h e)"), ident[:, :])
                    tr.then_inc(chunk_ok, 1)
                elif c[0] == "logits":
                    g = c[1]
                    n = number[("x", 2 * g + 1)]
                    pe.wait_ge(hi_ok, n + 1)
                    pe.wait_ge(lo_ok, lows(n + 1))
                    if g >= 2:
                        pe.wait_ge(lg_ok, g - 1)
                    for t in tiles(g):
                        o = logits(t)
                        mms = [(a[:, kd, P * t:P * t + P], gateT[:, kd, :]) for kd in range(KD) for a in (xT_hi, xT_lo)]
                        for m, (a, b) in enumerate(mms):
                            mm = pe.matmul(o, a, b, start=(m == 0), stop=(m == len(mms) - 1))
                    mm.then_inc(logits_ok, 1)
                elif c[0] == "qkv":
                    project(c[1])
                elif c[0] == "slots":
                    pe.wait_ge(slots_ok, 1)
                    pe.transpose(ps[:, B_SLOTS, 0:E], slots[:, :, :].rearrange("e two c -> e (two c)"),
                                 ident[0:E, 0:E]).then_inc(slotsT_ok, 1)


            def gx_transposes(i):
                pe.wait_ge(gx_in[i % 4], 16 * (i // 4 + 1))
                if i:
                    pe.wait_ge(gxT_ok, i)
                if i >= 3:
                    pe.wait_ge(hidT_ok, i - 2)
                for kd in range(KD):
                    tr = pe.transpose(ps[:, B_GXT, 0:D][:, P * kd:P * kd + P], gx[:, i % 4, kd:D:KD], ident[:, :])
                tr.then_inc(gtr_ok, 1)

            def shared_up(g, b):
                if b == 0 and g == 0:
                    pe.wait_ge(qkv_copied, NT)
                elif b == 0:
                    pe.wait_ge(shid_ok, 2 * g)
                cols = slice(SH0 + P * b, SH0 + P * b + P)
                mms = [(w[:, kd, cols], xx[:, kd, GT * g:GT * g + GT])
                       for kd in range(KD) for w, xx in passes(wT_hi, wT_lo, xT_hi, xT_lo)]
                for m, (a, r) in enumerate(mms):
                    mm = pe.matmul(ps[:, B_SH[b], :], a, r, start=(m == 0), stop=(m == len(mms) - 1))
                mm.then_inc(shup_ok, 1)

            def shared_down(t2):
                g = t2 // 2
                pe.wait_ge(shhi_ok, 2 * g + 2)
                pe.wait_ge(shlo_ok, 2 * g + 2)
                if t2:
                    pe.wait_ge(shadd_ok, t2)
                else:
                    pe.wait_ge(acol_ok, 1)
                for half in range(2):
                    j = 2 * (t2 % 2) + half
                    mms = [(a[0:n, kt, P * j:P * j + P], b[0:n, kt, :])
                           for kt, n in ((0, P), (1, SI - P)) for a, b in passes(sh_hi, sh_lo, sdT_hi, sdT_lo)]
                    for m, (a, b) in enumerate(mms):
                        mm = pe.matmul(ps[:, B_SHD, D * half:D * half + D], a, b, start=(m == 0), stop=(m == len(mms) - 1))
                mm.then_inc(shd_ok, 1)

            def q_transposes(t):
                pe.wait_ge(qrot_ok, t + 1)
                pe.wait_ge(shid_ok, 2 * NG)
                if t >= 2:
                    pe.wait_ge(qhi_ok, t - 1)
                    pe.wait_ge(qlo_ok, t - 1)
                for kd in range(KD):
                    tr = pe.transpose(ps[:, B_QT[t % 2], 0:D][:, P * kd:P * kd + P], q[:, t, P * kd:P * kd + P], ident[:, :])
                tr.then_inc(qt_ok, 1)

            def dense(t):
                pe.wait_ge(qlo_ok, t + 1)
                pe.wait_ge(woa_ok, 1 + t // SEQ_TILES)
                if t == 1:
                    pe.wait_ge(shadd_ok, NT // 2)
                if t >= 2:
                    pe.wait_ge(dadd_ok, t - 1)
                s = t // SEQ_TILES
                mms = [(ones[:, :], bias_hl[:, QKV:QKV + D])]
                mms += [(a[:, t % 2, kd, :], b[:, s, kd, :])
                        for kd in range(KD) for a, b in passes(qT_hi, qT_lo, woA_hi, woA_lo)]
                for m, (a, b) in enumerate(mms):
                    mm = pe.matmul(ps[:, B_OUT[t % 2], 0:D], a, b, start=(m == 0), stop=(m == len(mms) - 1))
                mm.then_inc(dense_ok, 1)

            pe.wait_ge(hi_ok, len(chunks))
            pe.wait_ge(index_ok, 1)

            def up(i):
                pe.wait_ge(gxT_ok, i + 1)
                pe.wait_ge(gu_in[i % NW], 16 * (i // NW + 1))
                if i:
                    pe.wait_ge(hid_ok, i)
                for kd in range(KD):
                    for e in range(2):
                        mm = pe.matmul(ps[CAP * e:CAP * e + CAP, B_H, 0:2 * I], gxT[:, i % 2, kd, CAP * e:CAP * e + CAP],
                                       gu[:, i % NW, e, kd, :], start=(kd == 0), stop=(kd == KD - 1))
                mm.then_inc(up_ok, 1)

            gx_transposes(0)
            up(0)
            gx_transposes(1)
            for i in range(NP):
                if i + 2 < NP:
                    gx_transposes(i + 2)
                pe.wait_ge(hid_ok, i + 1)
                pe.transpose(ps[0:I, B_GXT, D:D + P], hid[:, :], ident[:, :]).then_inc(ht_ok, 1)
                if i + 1 < NP:
                    up(i + 1)
                for f in FILL[i]:
                    if f[0] == "qkv":
                        project(f[1])
                    elif f == ("scale", 0):
                        for t in range(NT - LAG, NT):
                            a_sum(t)
                    elif f[0] == "up":
                        shared_up(f[1], f[2])
                    elif f[0] == "down":
                        shared_down(f[1])
                    elif f[0] == "qt":
                        q_transposes(f[1])
                        if f[1]:
                            dense(f[1] - 1)
                if i == NP - 1:
                    dense(NT - 1)
                pe.wait_ge(hidT_ok, i + 1)
                pe.wait_ge(dn_in[i % NW], 16 * (i // NW + 1))
                if i >= 2:
                    pe.wait_ge(eo_ok, i - 1)
                for e in range(2):
                    mm = pe.matmul(ps[CAP * e:CAP * e + CAP, B_EO[i % 2], 0:D], hidT[:, CAP * e:CAP * e + CAP],
                                   dn[:, i % NW, e, :], start=True, stop=True)
                mm.then_inc(down_ok, 1)

        @block.vector
        def _(dve):
            steps = [0]

            def step(ins):
                steps[0] += 1
                ins.then_inc(vstep, 1)
                return steps[0]

            def done(ins):
                dve.wait_ge(vstep, step(ins))

            def layer_stats(g):
                dve.wait_ge(x_in[g], 16)
                for t in tiles(g):
                    n = step(dve.bn_stats(stats[:, t, :], x[:, t, :]))
                dve.wait_ge(vstep, n)
                for t in tiles(g):
                    n = step(dve.bn_aggr(mv[:, t, :], stats[:, t, :]))
                dve.wait_ge(vstep, n)
                dve.tensor_scalar(var[:, TG * g:TG * g + TG], mv[:, TG * g:TG * g + TG, 1], EPS, None,
                                  ALU.add).then_inc(var_ok, 1)

            def minus_mean(g):
                s = slice(TG * g, TG * g + TG)
                dve.wait_ge(rstd_ok, g + 1)
                dve.scalar_tensor_tensor(out=nmr[:, s], in0=mv[:, s, 0], scalar=-1.0, in1=rstd[:, s],
                                         op0=ALU.mult, op1=ALU.mult).then_inc(nmr_ok, 1)

            def normalise(g):
                dve.wait_ge(rstd_ok, g + 1)
                dve.wait_ge(xn_ok, TG * g)
                for t in tiles(g):
                    dve.tensor_scalar(xn[:, t, :], x[:, t, :], mv[:, t, 0:1], rstd[:, t:t + 1],
                                      ALU.subtract, ALU.mult).then_inc(xn_ok, 1)

            def low_part(c):
                n = number[c]
                bank = ps[:, bank_of[c], :]
                dve.wait_ge(hi_ok, n + 1)
                if c[0] == "gate":
                    dve.tensor_tensor(gateT[:, :, E:2 * E], bank[:, 0:KD * E].rearrange("p (k e) -> p k e", k=KD),
                                      gateT[:, :, 0:E].bitcast(F32), ALU.subtract).then_inc(lo_ok, 1)
                else:
                    g, kd = c[1] // 2, c[1] % 2
                    s = slice(GT * g, GT * g + GT)
                    dve.tensor_tensor(xT_lo[:, kd, s], bank, xT_hi[:, kd, s].bitcast(F32), ALU.subtract).then_inc(lo_ok, 1)

            def choose(g):
                dve.wait_ge(logits_ok, g + 1)
                if g >= 2:
                    dve.wait_ge(shifted_ok, TG * (g - 1))
                halves = ps[:, B_LOGITS[g % 2], :].rearrange("p (t h e) -> p t h e", h=2, e=E)
                done(dve.tensor_copy(lg[:, g % 2, :, :], halves[:, :, 0, :]))
                dve.tensor_tensor(lg[:, g % 2, :, :], lg[:, g % 2, :, :], halves[:, :, 1, :], ALU.add).then_inc(lg_ok, 1)
                dve.wait_ge(lg_ok, g + 1)
                for j, t in enumerate(tiles(g)):
                    n = step(dve.max(best[:, t, :], lg[:, g % 2, j, :]))
                dve.wait_ge(vstep, n)
                if g >= 2:
                    dve.wait_ge(exp_ok, TG * (g - 1))
                for j, t in enumerate(tiles(g)):
                    dve.tensor_scalar(shifted[:, g % 2, j, 0:E], lg[:, g % 2, j, :], best[:, t, 0:1], LOWEST,
                                      ALU.subtract, ALU.max).then_inc(shifted_ok, 1)
                s = slice(TG * g, TG * g + TG)
                done(dve.tensor_tensor(best_sh[:, :, 0:TOPK], best[:, s, 0:TOPK],
                                       best[:, s, 0:1].to_broadcast([P, TG, TOPK]), ALU.subtract))
                done(dve.tensor_scalar(best_sh[:, :, 0:TOPK], best_sh[:, :, 0:TOPK], LOWEST, None, ALU.max))
                dve.wait_ge(shifted_ok, TG * g + TG)
                for j in range(TG):
                    n = step(dve.match_replace(marked[:, j, :], best_sh[:, j, :], shifted[:, g % 2, j, :], CHOSEN))
                dve.wait_ge(vstep, n)
                j0 = TG * g % SEQ_TILES
                dve.scalar_tensor_tensor(out=key[:, j0:j0 + TG, g // 2, :], in0=marked[:, :, 0:E], scalar=CHOSEN,
                                         in1=kconst[:, s].unsqueeze(2).to_broadcast([P, TG, E]),
                                         op0=ALU.is_equal, op1=ALU.mult).then_inc(marked_ok, 1)

            def invert_sums(g):
                s = slice(TG * g, TG * g + TG)
                dve.wait_ge(exp_ok, TG * g + TG)
                dve.reciprocal(einv[:, s], esum[:, s]).then_inc(einv_ok, 1)

            dve.memset(zeros[:, :], 0.0).then_inc(vconst_ok, 1)
            n = step(dve.memset(shifted[:, :, :, E:E + 2], PADDED))
            n = step(dve.memset(best_sh[:, :, TOPK:8], PADDED))
            dve.memset(bias_hl[:, :].bitcast(F32), 0.0).then_inc(vconst_ok, 1)
            n = step(dve.memset(ones[:, :].bitcast(F32), 1.0))
            dve.wait_ge(iota_ok, 1)
            n = step(dve.tensor_copy(kconst[:, :], kconst_i[:, :]))
            n = step(dve.tensor_copy(cpart[:, :], cpart_i[:, :]))
            dve.wait_ge(vstep, n)

            layer_stats(0)
            layer_stats(1)
            minus_mean(0)
            layer_stats(2)
            minus_mean(1)
            low_part(("gate", 0))
            low_part(("x", 0))
            low_part(("x", 1))
            layer_stats(3)
            minus_mean(2)
            low_part(("x", 2))
            low_part(("x", 3))
            normalise(3)
            choose(0)
            low_part(("x", 4))
            low_part(("x", 5))
            choose(1)
            low_part(("x", 6))
            low_part(("x", 7))
            invert_sums(0)
            choose(2)
            invert_sums(1)
            choose(3)
            invert_sums(2)
            invert_sums(3)

            dve.wait_ge(hi_ok, number[("key", 1)] + 1)
            for r in range(CAP // 8):
                done(dve.max(cand[:, 8 * r:8 * r + 8], keyT[:, :]))
                if r + 1 < CAP // 8:
                    done(dve.match_replace(keyT[:, :], cand[:, 8 * r:8 * r + 8], keyT[:, :], -1.0))
            done(dve.tensor_copy(other[:, :], cand[E:2 * E, ::-1]))
            for copy in range(2):
                n = step(dve.tensor_tensor(slots[:, copy, :], cand[0:E, :], other[:, :], ALU.max))
            dve.wait_ge(vstep, n)
            dve.sem_inc(slots_ok, 1)

            dve.wait_ge(slotsT_ok, 1)
            slotsT = ps[:, B_SLOTS, 0:E].rearrange("c (i two) -> c i two", two=2)
            n = step(dve.tensor_copy(keyc[0:CAP, :], slotsT[0:CAP, :, 0]))
            done(dve.tensor_copy(keyc[CAP:P, :], slotsT[CAP:P, :, 1]))
            n = step(dve.tensor_scalar(tokf[:, :], keyc[:, :], -1.0, float(T), ALU.mult, ALU.add))
            done(dve.tensor_scalar(padc[:, :], keyc[:, :], 0.0, cpart[:, :], ALU.is_equal, ALU.mult))
            n = step(dve.tensor_scalar(from_row[:, :], tokf[:, :], float(T - 1), None, ALU.min))
            done(dve.scalar_tensor_tensor(out=to_row[:, :], in0=padc[:, :], scalar=base[:, :], in1=keyc[:, :],
                                          op0=ALU.add, op1=ALU.subtract))
            dve.sem_inc(index_ok, 1)

            def scale_wout(s):
                if s == 0:
                    dve.wait_ge(a_ok, NT)
                    dve.wait_ge(hi_ok, number[("wo", 0)] + 1)
                    dve.tensor_copy(acol[:, :], ps[:, B_A, 0:4]).then_inc(acol_ok, 1)
                    dve.wait_ge(acol_ok, 1)
                for kd in range(KD):
                    a = acol[:, 2 * s + kd:2 * s + kd + 1]
                    n = step(dve.tensor_scalar(woA[:, s, kd, :], woT[:, kd, :], a, None, ALU.mult))
                dve.wait_ge(vstep, n)
                done(dve.tensor_copy(woA_hi[:, s, :, :], woA[:, s, :, :]))
                dve.tensor_tensor(woA_lo[:, s, :, :], woA[:, s, :, :], woA_hi[:, s, :, :].bitcast(F32),
                                  ALU.subtract).then_inc(woa_ok, 1)

            dve.wait_ge(table_in, 32)
            dve.wait_ge(kv_ok, POOL_T)
            for t in range(POOL_T, EARLY_T):
                rotate_k(dve, done, t)

            def take_scores(i):
                dve.wait_ge(gx_in[i % 4], 16 * (i // 4 + 1))
                if i >= 4:
                    dve.wait_ge(hid_ok, i - 3)
                for e in range(2):
                    s = slice(CAP * e, CAP * e + CAP)
                    dve.tensor_copy(wsl[s, i % 4:i % 4 + 1], gx[s, i % 4, D + 2 * i + e:D + 2 * i + e + 1]).then_inc(wsl_ok, 1)

            def hidden(i):
                dve.wait_ge(sg_ok, i + 1)
                dve.wait_ge(wsl_ok, 2 * i + 2)
                if i:
                    dve.wait_ge(ht_ok, i)
                dve.scalar_tensor_tensor(out=hid[:, :], in0=sg[:, :], scalar=wsl[:, i % 4:i % 4 + 1],
                                         in1=ps[:, B_H, I:2 * I], op0=ALU.mult, op1=ALU.mult).then_inc(hid_ok, 1)

            def output(i):
                dve.wait_ge(down_ok, i + 1)
                if i >= 4:
                    dve.wait_ge(scattered, 16 * (i - 3))
                dve.tensor_copy(eo[:, i % 4, :], ps[:, B_EO[i % 2], 0:D]).then_inc(eo_ok, 1)

            def add_dense(t):
                dve.wait_ge(dense_ok, t + 1)
                dve.wait_ge(shadd_ok, NT // 2)
                dve.tensor_tensor(x[:, t, :], ps[:, B_OUT[t % 2], 0:D], x[:, t, :], ALU.add).then_inc(dadd_ok, 1)

            take_scores(0)
            take_scores(1)
            hidden(0)
            for i in range(NP):
                if i:
                    output(i - 1)
                for f in FILL[i - 1] if i else []:
                    if f[0] == "qkv":
                        rotate_k(dve, done, f[1])
                    elif f[0] == "scale":
                        scale_wout(f[1])
                    elif f[0] == "down":
                        t2 = f[1]
                        xx = x[:, 2 * t2:2 * t2 + 2, :]
                        dve.wait_ge(shd_ok, t2 + 1)
                        dve.wait_ge(resid_ok, NG)
                        dve.tensor_tensor(xx, ps[:, B_SHD, :].rearrange("p (n d) -> p n d", n=2), xx,
                                          ALU.add).then_inc(shadd_ok, 1)
                if i + 2 < NP:
                    take_scores(i + 2)
                if i + 1 < NP:
                    hidden(i + 1)
                for f in FILL[i]:
                    if f[0] == "rotq":
                        t = f[1]
                        dve.wait_ge(qkv_copied, t + 1)
                        if t:
                            dve.wait_ge(qrot_ok, t)
                        rotate(dve, done, q[:, t, :], rot_q, *tables(t)).then_inc(qrot_ok, 1)
                    elif f[0] == "hid":
                        g = f[1]
                        dve.wait_ge(silu_ok, 2 * g + 1)
                        if g:
                            dve.wait_ge(shhi_ok, 2 * g)
                            dve.wait_ge(shlo_ok, 2 * g)
                        dve.tensor_tensor(sh_hid[:, 0, :], sh_sg[:, 0, :], ps[:, B_SH[2], :], ALU.mult).then_inc(shid_ok, 1)
                        dve.wait_ge(silu_ok, 2 * g + 2)
                        dve.tensor_tensor(sh_hid[0:SI - P, 1, :], sh_sg[0:SI - P, 1, :], ps[SI - P:P, B_SH[1], :],
                                          ALU.mult).then_inc(shid_ok, 1)
                    elif f[0] == "split":
                        g = f[1]
                        dve.wait_ge(shhi_ok, 2 * g + 1)
                        if g:
                            dve.wait_ge(shd_ok, 2 * g)
                        dve.tensor_tensor(sh_lo[:, 0, :], sh_hid[:, 0, :], sh_hi[:, 0, :].bitcast(F32),
                                          ALU.subtract).then_inc(shlo_ok, 1)
                        dve.wait_ge(shhi_ok, 2 * g + 2)
                        dve.tensor_tensor(sh_lo[0:SI - P, 1, :], sh_hid[0:SI - P, 1, :],
                                          sh_hi[0:SI - P, 1, :].bitcast(F32), ALU.subtract).then_inc(shlo_ok, 1)
                    elif f[0] == "qt":
                        t = f[1]
                        dve.wait_ge(qhi_ok, t + 1)
                        if t >= 2:
                            dve.wait_ge(dense_ok, t - 1)
                        dve.tensor_tensor(qT_lo[:, t % 2, :, :], ps[:, B_QT[t % 2], 0:D].rearrange("p (k c) -> p k c", k=KD),
                                          qT_hi[:, t % 2, :, :].bitcast(F32), ALU.subtract).then_inc(qlo_ok, 1)
                        if t >= 2:
                            add_dense(t - 2)
            add_dense(NT - 2)
            output(NP - 1)
            add_dense(NT - 1)

            dve.wait_ge(dadd_ok, NT)
            for n in range(NT // PART):
                s = slice(PART * n, PART * n + PART)
                dve.wait_ge(sum_in[n], 32)
                dve.tensor_tensor(x[:, s, :], x[:, s, :], q[:, s, :], ALU.add).then_inc(half_sum, 1)
                dve.wait_ge(half_sum, n + 1)
                dve.tensor_tensor(x[:, s, :], x[:, s, :], w_raw[:, PART * (n % 4):PART * (n % 4) + PART, :],
                                  ALU.add).then_inc(total_ok, 1)


_INS = ['L0_attn_X', 'L0_attn_W_in', 'L0_attn_b_in', 'L0_attn_W_out', 'L0_attn_b_out', 'L0_ffn_gate_w',
        'L0_ffn_gate_up_proj', 'L0_ffn_down_proj', 'L0_ffn_shared_gate_w', 'L0_ffn_shared_up_w',
        'L0_ffn_shared_down_w']
_OUTS = [((2, 1024, 256), 'float32')]


def rope_tables(seq, rot):
    import numpy as _np
    inv = (1.0 / _np.float32(10000.0) ** (_np.arange(0, rot, 2, dtype=_np.float32) / _np.float32(rot))).astype(_np.float32)
    angle = _np.repeat(_np.arange(seq, dtype=_np.float32)[:, None] * inv[None, :], 2, axis=-1)
    sign = _np.where(_np.arange(rot) % 2 == 0, _np.float32(-1), _np.float32(1))
    return _np.cos(angle).astype(_np.float32), (_np.sin(angle) * sign).astype(_np.float32)


def kernel(**inputs):
    import numpy as _np
    import concourse.bacc as _bacc
    from concourse import mybir as _mybir
    from concourse.bass_utils import run_bass_kernel_spmd as _run

    nc = _bacc.Bacc("TRN2", target_bir_lowering=False, num_devices=1)
    arrays, args = {}, []
    named = [(name, _np.ascontiguousarray(inputs[name])) for name in _INS]
    named += list(zip(("cos_table", "sin_table"), rope_tables(1024, 128)))
    for name, a in named:
        arrays[f"in_{name}_dram"] = a
        args.append(nc.dram_tensor(f"in_{name}_dram", a.shape, _mybir.dt.from_np(a.dtype), kind="ExternalInput").ap())
    for i, (shape, dtype) in enumerate(_OUTS):
        dt = _mybir.dt.from_np(_np.dtype(dtype))
        args.append(nc.dram_tensor(f"out_{i}_dram", shape, dt, kind="ExternalOutput").ap())
    rows = nc.dram_tensor("token_rows", (T, ROW), _mybir.dt.float32, kind="Internal").ap()
    sums = nc.dram_tensor("expert_sums", (2 * SUMROWS, D), _mybir.dt.float32, kind="Internal").ap()
    build(nc, *args, rows, sums)
    r = _run(nc, [arrays], core_ids=[0])
    return r.results[0]["out_0_dram"]
```

```python
from contextlib import ExitStack

import concourse.bass as bass
from concourse import mybir

F32 = mybir.dt.float32
F32R = mybir.dt.float32r
U32 = mybir.dt.uint32
I32 = mybir.dt.int32
ALU = mybir.AluOpType
ACT = mybir.ActivationFunctionType
AX_X = mybir.AxisListType.X

P = 128
D = 256
KD = D // P
T = 2048
NT = T // P
NG = 4
TG = NT // NG
GT = TG * P
SEQ_TILES = NT // 2
ROT = D // 2
E = 64
TOPK = 6
CAP = 64
I = 96
SI = 2 * I
NP = E // 2
NW = 3
ROW = D + E
SUMROWS = T + CAP
QKV = 3 * D
SH0 = QKV
WCOLS = SH0 + 2 * SI
EPS = 1e-5
LOWEST = -87.3
PADDED = 1.0
CHOSEN = 2.0
EARLY_T = 11
POOL_T = 7
SLOTS_T = 8
WARM_UP = 44
SCALE_AT = (4, 8)
PART = 2
RING = 6

B_CHUNK = (0, 1)
B_CHUNK6 = (0, 1, 4, 5, 6, 7)
B_LOGITS = (2, 3)
B_SLOTS = 3
B_GXT = 0
B_H = 1
B_EO = (2, 3)
B_QK = (4, 5)
B_V = 6
B_A = 7
B_SH = (4, 5, 6)
B_SHD = 7
B_QT = (4, 5)
B_OUT = (6, 7)

FILL = [[] for _ in range(NP)]
_at = 1
for _t in range(EARLY_T, NT):
    FILL[_at] += [("qkv", _t)]
    _at += 1
FILL[_at + SCALE_AT[0]] += [("scale", 0)]
FILL[_at + SCALE_AT[1]] += [("scale", 1)]
for _g in range(NG):
    for _b in range(3):
        FILL[_at + 4 * _g + _b] += [("up", _g, _b)]
    FILL[_at + 4 * _g + 3] += [("hid", _g)]
    FILL[_at + 4 * _g + 4] += [("split", _g)]
    _i = _at + 4 * _g + (6 if _g < NG - 1 else 5)
    FILL[_i] += [("down", 2 * _g)]
    FILL[_i + 1] += [("down", 2 * _g + 1)]
_at += 4 * NG + 2
for _t in range(NT):
    FILL[_t] += [("rotq", _t)]
    FILL[_at + _t * (NP - _at) // NT] += [("qt", _t)]


def build(nc, X, W_in, b_in, W_out, b_out, gate_w, gate_up, down, sh_gate, sh_up, sh_down,
          cos_t, sin_t, out, rows, sums):
    x_d = X.rearrange("b s d -> (b s) d").rearrange("(n p) d -> p n d", p=P)
    out_d = out.rearrange("b s d -> (b s) d").rearrange("(n p) d -> p n d", p=P)
    rows_d = rows.rearrange("(n p) c -> p n c", p=P)

    order = [("norm", 0), ("gate", 0), ("x", 0), ("x", 1), ("norm", 1), ("logits", 0), ("lcopy", 0), ("x", 2), ("x", 3)]
    order += [("resid", 0), ("tok", 0), ("norm", 2), ("logits", 1), ("resid", 1), ("x", 4), ("x", 5), ("lcopy", 1), ("bias", 0), ("x", 6), ("x", 7)]
    order += [("tok", 1), ("exp", 0), ("w", 0), ("w", 1), ("logits", 2), ("lcopy", 2), ("w", 2), ("exp", 1), ("tok", 2)]
    order += [("logits", 3), ("lcopy", 3), ("tok", 3), ("resid", 2), ("exp", 2), ("resid", 3), ("qkv", 0)]
    order += [("key", 0), ("key", 1), ("exp", 3), ("qkv", 1), ("w", 3), ("qkv", 2), ("w", 4), ("qkv", 3), ("sd", 0)]
    order += [("qkv", 4), ("wo", 0), ("qkv", 5)]
    order += [("qkv", t) for t in range(6, SLOTS_T)] + [("slots", 0)] + [("qkv", t) for t in range(SLOTS_T, EARLY_T - 1)]
    act_order = [c for c in order if c != ("qkv", 0)]
    act_order.insert(act_order.index(("exp", 3)) + 1, ("qkv", 0))
    chunks = [c for c in order if c[0] in ("gate", "x", "w", "key", "sd", "wo")]
    number = {c: n for n, c in enumerate(chunks)}
    before_qkv = [c for c in order[:order.index(("qkv", 0))] if c in number]
    bank_of = {c: B_CHUNK6[n % 6] if c in before_qkv else B_CHUNK[n % 2] for n, c in enumerate(chunks)}
    freed = {c: max([m + 1 for m, d in enumerate(chunks[:n]) if bank_of[d] == bank_of[c]], default=0)
             for n, c in enumerate(chunks)}

    def lows(n):
        return sum(c[0] in ("gate", "x") for c in chunks[:n])

    with ExitStack() as ctx:
        def sb(name, shape, dt=F32):
            return ctx.enter_context(nc.sbuf_tensor(name, shape, dt))

        def sem(name):
            return ctx.enter_context(nc.semaphore(name))

        x = sb("x", [P, NT, D])
        scores = sb("scores", [P, NT, E])
        xT_hi = sb("xT_hi", [P, KD, T], F32R)
        xT_lo = sb("xT_lo", [P, KD, T], F32R)
        w_raw = sb("w_raw", [P, 12, D])
        sd_raw = sb("sd_raw", [P, KD, SI])
        wT_hi = sb("wT_hi", [P, KD, WCOLS], F32R)
        wT_lo = sb("wT_lo", [P, KD, WCOLS], F32R)
        gateT = sb("gateT", [P, KD, 2 * E], F32R)
        sel = sb("sel", [P, E])
        woT = sb("woT", [P, KD, D])
        woA = sb("woA", [P, 2, KD, D])
        woA_hi = sb("woA_hi", [P, 2, KD, D], F32R)
        woA_lo = sb("woA_lo", [P, 2, KD, D], F32R)
        sdT_hi = sb("sdT_hi", [P, 2, D], F32R)
        sdT_lo = sb("sdT_lo", [P, 2, D], F32R)
        ident = sb("ident", [P, P])
        ones = sb("ones", [P, P], F32R)
        bias_hl = sb("bias_hl", [P, QKV + D], F32R)
        cos = sb("cos", [P, SEQ_TILES, ROT])
        sin = sb("sin", [P, SEQ_TILES, ROT])
        stats = sb("stats", [P, NT, 6])
        mv = sb("mv", [P, NT, 2])
        var = sb("var", [P, NT])
        rstd = sb("rstd", [P, NT])
        nmr = sb("nmr", [P, NT])
        minus_half = sb("minus_half", [P, TG])
        kconst_i = sb("kconst_i", [P, NT], I32)
        kconst = sb("kconst", [P, NT])
        cpart_i = sb("cpart_i", [P, 1], I32)
        cpart = sb("cpart", [P, 1])
        base = sb("base", [P, 1])
        base_last = sb("base_last", [P, 1])
        to_last = sb("to_last", [CAP, 1], U32)
        best = sb("best", [P, NT, 8])
        best_sh = sb("best_sh", [P, TG, 8])
        shifted = sb("shifted", [P, 2, TG, E + 2])
        marked = sb("marked", [P, TG, E + 2])
        expo = sb("expo", [P, 2, TG, E])
        esum = sb("esum", [P, NT])
        einv = sb("einv", [P, NT])
        cand = sb("cand", [P, CAP])
        other = sb("other", [E, CAP])
        slots = sb("slots", [E, 2, CAP])
        keyc = sb("keyc", [P, NP])
        tokf = sb("tokf", [P, NP])
        padc = sb("padc", [P, NP])
        from_row = sb("from_row", [P, NP], U32)
        to_row = sb("to_row", [P, NP], U32)
        q = sb("q", [P, NT, D])
        k = sb("k", [P, 3, D])
        v = sb("v", [P, 3, D])
        ksq = sb("ksq", [P, D])
        rot_q = sb("rot_q", [P, 2, ROT])
        rot_k = sb("rot_k", [P, 2, ROT])
        acc = sb("acc", [P, 2, D])
        kv = sb("kv", [P, POOL_T, D])
        ss = sb("ss", [P, NT])
        ssm = sb("ssm", [P, NT])
        rnorm = sb("rnorm", [P, NT])
        acol = sb("acol", [P, 4])
        sh_sg = sb("sh_sg", [P, 2, GT])
        sh_hid = sb("sh_hid", [P, 2, GT])
        sh_hi = sb("sh_hi", [P, 2, GT], F32R)
        sh_lo = sb("sh_lo", [P, GT], F32R)
        sh_hi1 = sb("sh_hi1", [P, GT], F32R)
        qT_hi = sb("qT_hi", [P, 2, KD, P], F32R)
        qT_lo = sb("qT_lo", [P, 2, KD, P], F32R)
        gu = sb("gu", [P, NW, 2, KD, 2 * I])
        dn = sb("dn", [I, NW, 2, D])
        gx = sb("gx", [P, 4, ROW])
        gxT = sb("gxT", [P, 2, KD, P])
        sg = sb("sg", [P, I])
        hid = sb("hid", [P, I])
        hidT = sb("hidT", [I, P])
        wsl = sb("wsl", [P, 4])
        eo = sb("eo", [P, 4, D])
        spare = sb("spare", [P, 1])
        zeros = sb("zeros", [P, D])
        w_stage = sh_hid
        lgT = eo[:, :, :].rearrange("p (g r) d -> p g (r d)", g=2)
        xn = q
        bias = gx[:, :, :].rearrange("p r c -> p (r c)")[:, 0:QKV + D]
        key = woA[:, :, :, :].rearrange("p s k d -> p (s k d)").rearrange("p (j h e) -> p j h e", h=2, e=E)
        keyT = eo[:, :, :].rearrange("p r d -> p (r d)")

        ps = ctx.enter_context(nc.psum_tensor("ps", [P, 8, 512], F32))

        x_in = [sem(f"x_in{g}") for g in range(NG)]
        gate_in = sem("gate_in")
        win_in = sem("win_in")
        wout_in = sem("wout_in")
        sh_in = sem("sh_in")
        sd_in = sem("sd_in")
        table_in = sem("table_in")
        bias_in = sem("bias_in")
        ident_ok = sem("ident_ok")
        iota_ok = sem("iota_ok")
        vconst_ok = sem("vconst_ok")
        vstep = sem("vstep")
        gstep = sem("gstep")
        var_ok = sem("var_ok")
        rstd_ok = sem("rstd_ok")
        nmr_ok = sem("nmr_ok")
        xn_ok = sem("xn_ok")
        resid_ok = sem("resid_ok")
        chunk_ok = sem("chunk_ok")
        hi_ok = sem("hi_ok")
        lo_ok = sem("lo_ok")
        wlo_ok = sem("wlo_ok")
        logits_ok = sem("logits_ok")
        lgT_ok = sem("lgT_ok")
        lcopy_ok = sem("lcopy_ok")
        sel_ok = sem("sel_ok")
        shifted_ok = sem("shifted_ok")
        exp_ok = sem("exp_ok")
        einv_ok = sem("einv_ok")
        marked_ok = sem("marked_ok")
        scores_ok = sem("scores_ok")
        xn_out = [sem(f"xn_out{g}") for g in range(NG)]
        scores_out = sem("scores_out")
        zero_out = sem("zero_out")
        bias_hi_ok = sem("bias_hi_ok")
        bias_ok = sem("bias_ok")
        sdb_ok = sem("sdb_ok")
        qkv_ok = sem("qkv_ok")
        qkv_copied = sem("qkv_copied")
        v_copied = sem("v_copied")
        qrot_ok = sem("qrot_ok")
        kv_ok = sem("kv_ok")
        rnorm_ok = sem("rnorm_ok")
        a_ok = sem("a_ok")
        aT_ok = sem("aT_ok")
        acol_ok = sem("acol_ok")
        woa_ok = sem("woa_ok")
        slots_ok = sem("slots_ok")
        slotsT_ok = sem("slotsT_ok")
        index_ok = sem("index_ok")
        shup_ok = sem("shup_ok")
        silu_ok = sem("silu_ok")
        shid_ok = sem("shid_ok")
        shhi_ok = sem("shhi_ok")
        shlo_ok = sem("shlo_ok")
        shd_ok = sem("shd_ok")
        shadd_ok = sem("shadd_ok")
        qt_ok = sem("qt_ok")
        qhi_ok = sem("qhi_ok")
        qlo_ok = sem("qlo_ok")
        dense_ok = sem("dense_ok")
        dadd_ok = sem("dadd_ok")
        gu_in = [sem(f"gu_in{r}") for r in range(NW)]
        dn_in = [sem(f"dn_in{r}") for r in range(NW)]
        gx_in = [sem(f"gx_in{r}") for r in range(4)]
        gtr_ok = sem("gtr_ok")
        gxT_ok = sem("gxT_ok")
        up_ok = sem("up_ok")
        sg_ok = sem("sg_ok")
        hid_ok = sem("hid_ok")
        ht_ok = sem("ht_ok")
        hidT_ok = sem("hidT_ok")
        wsl_ok = sem("wsl_ok")
        down_ok = sem("down_ok")
        eo_ok = sem("eo_ok")
        scattered = sem("scattered")
        sum_in = [sem(f"sum_in{g}") for g in range(NT // PART)]
        sum1_in = [sem(f"sum1_in{g}") for g in range(NT // PART)]
        half_sum = sem("half_sum")
        total_ok = sem("total_ok")
        out_done = sem("out_done")

        block = ctx.enter_context(nc.Block())

        def tiles(g):
            return range(TG * g, TG * g + TG)

        def logits(t):
            j = t % TG
            return ps[:, B_LOGITS[t // TG % 2], E * j:E * j + E]

        def w_cols(n):
            return slice(2 * P * n, min(2 * P * n + 2 * P, WCOLS))

        def rotate(eng, done, a, tmp, c, s):
            pairs = a[:, 0:ROT].rearrange("p (h two) -> p h two", two=2)
            done(eng.tensor_tensor(tmp[:, 0, :], a[:, 0:ROT], c, ALU.mult))
            done(eng.tensor_tensor(tmp[:, 1, :].rearrange("p (h two) -> p h two", two=2), pairs[:, :, ::-1],
                                   s.rearrange("p (h two) -> p h two", two=2), ALU.mult))
            return eng.tensor_tensor(a[:, 0:ROT], tmp[:, 0, :], tmp[:, 1, :], ALU.add)

        def tables(t):
            return cos[:, t % SEQ_TILES, :], sin[:, t % SEQ_TILES, :]

        def rotate_k(eng, done, t):
            eng.wait_ge(qkv_copied, t + 1)
            done(rotate(eng, done, k[:, t % 3, :], rot_k, *tables(t)))
            if t >= POOL_T:
                eng.wait_ge(a_ok, t - POOL_T + 1)
            eng.tensor_tensor(kv[:, t % POOL_T, :], k[:, t % 3, :], v[:, t % 3, :], ALU.mult).then_inc(kv_ok, 1)

        @block.sync
        def _(sp):
            sp.dma_start(w_raw[0:E, 11, :], gate_w).then_inc(gate_in, 16)
            for g in range(NG):
                sp.dma_start(x[:, TG * g:TG * g + TG, :], x_d[:, TG * g:TG * g + TG, :]).then_inc(x_in[g], 16)
            sp.dma_start(w_raw[:, 0:6, :], W_in.rearrange("(n p) d -> p n d", p=P)).then_inc(win_in, 16)
            sp.wait_ge(vconst_ok, 5)
            for b, n in ((b_in, 0), (b_out, QKV)):
                for r in (0, 32):
                    sp.dma_start(bias[r:r + 1, n:n + b.shape[0]], b.rearrange("(a n) -> a n", a=1)).then_inc(bias_in, 16)

            def weights(i):
                if i >= NW:
                    sp.wait_ge(up_ok, i - NW + 1)
                for e in range(2):
                    sp.dma_start(gu[:, i % NW, e, :, :],
                                 gate_up[2 * i + e].rearrange("(p k) n -> p k n", k=KD)).then_inc(gu_in[i % NW], 16)
                if i >= NW:
                    sp.wait_ge(down_ok, i - NW + 1)
                sp.dma_start(dn[:, i % NW, :, :], down[2 * i:2 * i + 2].rearrange("e i d -> i e d")).then_inc(dn_in[i % NW], 16)

            sums_p = sums.rearrange("(p n) d -> p n d", p=P)
            share = 2 * SUMROWS // P // 3
            for g in range(NG):
                sp.wait_ge(xn_ok, TG * g + TG)
                sp.dma_start(rows_d[:, TG * g:TG * g + TG, 0:D], xn[:, TG * g:TG * g + TG, :]).then_inc(xn_out[g], 16)
                if g == 0:
                    sp.dma_start(cos[:, :, :], cos_t.rearrange("(n p) d -> p n d", p=P)).then_inc(table_in, 16)
                    sp.dma_start(sin[:, :, :], sin_t.rearrange("(n p) d -> p n d", p=P)).then_inc(table_in, 16)
                elif g == 1:
                    sp.dma_start(w_raw[:, 8, :], sh_gate[0:P, :]).then_inc(sh_in, 16)
                    sp.dma_start(w_raw[0:SI - P, 9, :], sh_gate[P:SI, :]).then_inc(sh_in, 16)
                    sp.dma_start(w_raw[SI - P:P, 9, :], sh_up[P:SI, :]).then_inc(sh_in, 16)
                    sp.dma_start(w_raw[:, 10, :], sh_up[0:P, :]).then_inc(sh_in, 16)
                elif g == 2:
                    sp.dma_start(sd_raw[:, :, :], sh_down.rearrange("(n p) i -> p n i", p=P)).then_inc(sd_in, 16)
                    sp.dma_start(w_raw[:, 6:8, :], W_out.rearrange("(n p) d -> p n d", p=P)).then_inc(wout_in, 16)
            for n in range(NG):
                sp.wait_ge(scores_ok, n + 1)
                sp.dma_start(rows_d[:, TG * n:TG * n + TG, D:ROW], scores[:, TG * n:TG * n + TG, :]).then_inc(scores_out, 16)
            weights(0)
            weights(1)
            weights(2)
            sp.wait_ge(vconst_ok, 1)
            for n in range(3):
                sp.dma_start(sums_p[:, share * n:share * n + share, :],
                             zeros[:, None, :].to_broadcast([P, share, D])).then_inc(zero_out, 16)
            for i in range(NW, NP):
                weights(i)
            sums_d = sums.rearrange("(s r) d -> s r d", s=2)
            sp.wait_ge(scattered, 16 * (NP - 1))
            sp.wait_ge(qt_ok, NT)
            for n in range(NT // PART):
                if n >= 6:
                    sp.wait_ge(half_sum, n - 3)
                sp.dma_start(q[:, PART * n:PART * n + PART, :],
                             sums_d[0, PART * P * n:PART * P * (n + 1), :].rearrange("(n p) d -> p n d", p=P)).then_inc(sum_in[n], 16)
            sp.wait_ge(scattered, 16 * (NP + 1))
            for n in range(NT // PART):
                if n >= RING:
                    sp.wait_ge(total_ok, n - RING + 1)
                sp.dma_start(w_raw[:, PART * (n % RING):PART * (n % RING) + PART, :],
                             sums_d[1, PART * P * n:PART * P * (n + 1), :].rearrange("(n p) d -> p n d", p=P)).then_inc(sum1_in[n], 16)
            sp.wait_ge(out_done, 16 * NT // PART)

        @block.gpsimd
        def _(pool):
            steps = [0]

            def done(ins):
                steps[0] += 1
                ins.then_inc(gstep, 1)
                pool.wait_ge(gstep, steps[0])

            done(pool.memset(ident[:, :], 0.0))
            pool.affine_select(out=ident[:, :], in_=ident[:, :], compare_op=ALU.not_equal, fill=1.0, base=0,
                               pattern=[[-1, P]], channel_multiplier=1).then_inc(ident_ok, 1)
            pool.wait_ge(ident_ok, 1)
            done(pool.memset(minus_half[:, :], -0.5))
            done(pool.memset(base[0:P // 2, :], float(T)))
            done(pool.memset(base[P // 2:P, :], float(T + SUMROWS)))
            done(pool.memset(base_last[:, :], float(T + SUMROWS)))
            done(pool.iota(kconst_i[:, :], pattern=[[-P, NT]], base=T, channel_multiplier=-1))
            done(pool.iota(cpart_i[0:P // 2, :], pattern=[[0, 1]], base=0, channel_multiplier=1))
            pool.iota(cpart_i[P // 2:P, :], pattern=[[0, 1]], base=0, channel_multiplier=1).then_inc(iota_ok, 1)
            pool.wait_ge(iota_ok, 1)

            def rstds(g):
                pool.wait_ge(var_ok, g + 1)
                s = slice(TG * g, TG * g + TG)
                pool.tensor_tensor(rstd[:, s], var[:, s], minus_half[:, :], ALU.pow).then_inc(rstd_ok, 1)

            def residual(g):
                pool.wait_ge(xn_ok, TG * g + TG)
                s = slice(TG * g, TG * g + TG)
                pool.tensor_tensor(x[:, s, :], x[:, s, :], xn[:, s, :], ALU.add).then_inc(resid_ok, 1)

            def group_scores(g):
                pool.wait_ge(exp_ok, TG * g + TG)
                pool.wait_ge(einv_ok, g + 1)
                s = slice(TG * g, TG * g + TG)
                pool.tensor_tensor(scores[:, s, :], expo[:, g % 2, :, :],
                                   einv[:, s].unsqueeze(2).to_broadcast([P, TG, E]), ALU.mult).then_inc(scores_ok, 1)

            def weight_low(n, c):
                pool.wait_ge(hi_ok, number[c] + 1)
                stage = w_stage[:, n % 2, :]
                if c[0] == "w":
                    cols = w_cols(c[1])
                    m = cols.stop - cols.start
                    pool.tensor_tensor(wT_lo[:, :, cols], stage[:, 0:KD * m].rearrange("p (k m) -> p k m", k=KD),
                                       wT_hi[:, :, cols].bitcast(F32), ALU.subtract).then_inc(wlo_ok, 1)
                else:
                    st = stage.rearrange("p (k m) -> p k m", k=2)
                    done(pool.tensor_tensor(sdT_lo[:, 0, :], st[:, 0, :], sdT_hi[:, 0, :].bitcast(F32), ALU.subtract))
                    pool.tensor_tensor(sdT_lo[0:SI - P, 1, :], st[0:SI - P, 1, :],
                                       sdT_hi[0:SI - P, 1, :].bitcast(F32), ALU.subtract).then_inc(wlo_ok, 1)

            def inverse_norms(t, n):
                pool.wait_ge(qkv_copied, t + n)
                done(pool.tensor_scalar(ssm[:, t:t + n], ss[:, t:t + n], 1e-24, None, ALU.max))
                pool.tensor_tensor(rnorm[:, t:t + n], ssm[:, t:t + n], minus_half[:, 0:1].to_broadcast([P, n]),
                                   ALU.pow).then_inc(rnorm_ok, n)

            n_low = n_scores = n_resid = 0
            for g in range(NG):
                rstds(g)
            for c in order:
                if c[0] == "resid":
                    residual(c[1])
                    n_resid += 1
                elif c[0] == "exp":
                    group_scores(c[1])
                    n_scores += 1
                elif c[0] in ("w", "sd"):
                    weight_low(n_low, c)
                    n_low += 1
                elif c[0] == "bias":
                    pool.wait_ge(wlo_ok, n_low)
                    if n_scores:
                        pool.wait_ge(scores_ok, n_scores)
                    if n_resid:
                        pool.wait_ge(resid_ok, n_resid)
                    pool.wait_ge(bias_hi_ok, 1)
                    pool.tensor_tensor(bias_hl[32:33, :], bias[32:33, :], bias_hl[32:33, :].bitcast(F32),
                                       ALU.subtract).then_inc(bias_ok, 1)
                    pool.wait_ge(bias_ok, 1)
                elif c[0] == "qkv":
                    if c[1] == 0:
                        pool.wait_ge(table_in, 32)
                    if c[1] < POOL_T:
                        rotate_k(pool, done, c[1])
                        if c[1] == 3:
                            inverse_norms(0, 4)

            def gather(i):
                if i >= 4:
                    pool.wait_ge(gtr_ok, i - 3)
                    pool.wait_ge(wsl_ok, 2 * (i - 3))
                pool.indirect_dma_start(gx[:, i % 4, :], None, rows[:, :],
                                        bass.IndirectOffsetOnAxis(ap=from_row[:, i:i + 1], axis=0),
                                        bounds_check=T - 1, oob_is_err=False).then_inc(gx_in[i % 4], 16)

            pool.wait_ge(index_ok, 1)
            for g in range(NG):
                pool.wait_ge(xn_out[g], 16)
            pool.wait_ge(scores_out, 16 * NG)
            for i in range(4):
                gather(i)
            inverse_norms(4, POOL_T - 4)
            for t in range(POOL_T, EARLY_T, 2):
                inverse_norms(t, min(2, EARLY_T - t))
            gather(4)
            gather(5)
            pool.wait_ge(zero_out, 48)
            for i in range(NP):
                if i + 6 < NP:
                    gather(i + 6)
                for f in FILL[i - 1] if i else []:
                    if f[0] == "qkv":
                        inverse_norms(f[1], 1)
                pool.wait_ge(eo_ok, i + 1)
                if i:
                    pool.wait_ge(scattered, 16 * i)
                parts = [(slice(0, P), to_row[:, i:i + 1])]
                if i == NP - 1:
                    parts = [(slice(0, CAP), to_row[0:CAP, i:i + 1]), (slice(CAP, P), to_last[:, :])]
                for at, index in parts:
                    if at.start:
                        pool.wait_ge(scattered, 16 * NP)
                    pool.indirect_dma_start(sums[:, :], bass.IndirectOffsetOnAxis(ap=index, axis=0),
                                            eo[at, i % 4, :], None, bounds_check=2 * SUMROWS - 1, oob_is_err=True,
                                            compute_op=ALU.add).then_inc(scattered, 16)
            pool.wait_ge(scattered, 16 * (NP + 1))

        @block.scalar
        def _(act):
            def qkv_copy(t):
                act.wait_ge(qkv_ok, t + 1)
                bank = ps[:, B_QK[t % 2], :]
                act.wait_ge(xn_out[t // TG], 16)
                act.wait_ge(resid_ok, t // TG + 1)
                act.activation(q[:, t, :], bank[:, 0:D], ACT.Copy)
                if t >= 3:
                    act.wait_ge(kv_ok, t - 2)
                act.activation(k[:, t % 3, :], bank[:, D:2 * D], ACT.Copy)
                act.activation(v[:, t % 3, :], ps[:, B_V, 0:D], ACT.Copy).then_inc(v_copied, 1)
                if t:
                    act.wait_ge(qkv_copied, t)
                act.activation(ksq[:, :], bank[:, D:2 * D], ACT.Square,
                               accum_out=ss[:, t:t + 1]).then_inc(qkv_copied, 1)

            n_low = 0
            for c in act_order:
                if c[0] in ("gate", "x", "w", "key", "sd", "wo"):
                    n = number[c]
                    bank = ps[:, bank_of[c], :]
                    act.wait_ge(chunk_ok, n + 1)
                if c[0] == "norm":
                    act.wait_ge(nmr_ok, c[1] + 1)
                    for t in tiles(c[1]):
                        act.activation(xn[:, t, :], x[:, t, :], ACT.Identity, bias=nmr[:, t:t + 1],
                                       scale=rstd[:, t:t + 1]).then_inc(xn_ok, 1)
                elif c[0] == "gate":
                    act.activation(gateT[:, :, 0:E], bank[:, 0:KD * E].rearrange("p (k e) -> p k e", k=KD),
                                   ACT.Copy).then_inc(hi_ok, 1)
                elif c[0] == "x":
                    g, kd = c[1] // 2, c[1] % 2
                    act.activation(xT_hi[:, kd, GT * g:GT * g + GT], bank, ACT.Copy).then_inc(hi_ok, 1)
                elif c[0] == "w":
                    cols = w_cols(c[1])
                    m = cols.stop - cols.start
                    if n_low >= 2:
                        act.wait_ge(wlo_ok, n_low - 1)
                    act.activation(w_stage[:, n_low % 2, 0:KD * m], bank[:, 0:KD * m], ACT.Copy)
                    act.activation(wT_hi[:, :, cols], bank[:, 0:KD * m].rearrange("p (k m) -> p k m", k=KD),
                                   ACT.Copy).then_inc(hi_ok, 1)
                    n_low += 1
                elif c[0] == "lcopy":
                    g = c[1]
                    act.wait_ge(lgT_ok, g + 1)
                    if g >= 2:
                        act.wait_ge(logits_ok, g - 1)
                    act.activation(lgT[:, g % 2, :], ps[:, B_LOGITS[g % 2], :], ACT.Copy).then_inc(lcopy_ok, 1)
                elif c[0] == "bias":
                    act.wait_ge(bias_in, 64)
                    act.wait_ge(vconst_ok, 5)
                    act.activation(bias_hl[0:33, :], bias[0:33, :], ACT.Copy).then_inc(bias_hi_ok, 1)
                elif c[0] == "sd":
                    act.wait_ge(wlo_ok, n_low - 1)
                    b2 = bank.rearrange("p (k m) -> p k m", k=2)
                    st = w_stage[:, n_low % 2, :].rearrange("p (k m) -> p k m", k=2)
                    act.activation(st[:, 0, :], b2[:, 0, :], ACT.Copy)
                    act.activation(st[0:SI - P, 1, :], b2[0:SI - P, 1, :], ACT.Copy)
                    act.activation(sdT_hi[:, 0, :], b2[:, 0, :], ACT.Copy)
                    act.activation(sdT_hi[SI - P:P, 1, :], b2[0:SI - P, 1, :], ACT.Copy)
                    act.activation(sdT_hi[0:SI - P, 1, :], b2[0:SI - P, 1, :], ACT.Copy).then_inc(hi_ok, 1)
                    act.wait_ge(bias_ok, 1)
                    act.wait_ge(vconst_ok, 5)
                    for row in (0, 32):
                        act.activation(sdT_lo[SI - P + row:SI - P + row + 1, 1, :], bias_hl[row:row + 1, QKV:QKV + D],
                                       ACT.Copy).then_inc(sdb_ok, 1)
                    n_low += 1
                    act.activation(spare[:, :], ident[:, 0:1], ACT.Silu)
                elif c[0] == "wo":
                    act.activation(woT[:, :, :], bank.rearrange("p (k m) -> p k m", k=KD), ACT.Copy).then_inc(hi_ok, 1)
                elif c[0] == "key":
                    act.activation(keyT[:, 4 * P * c[1]:4 * P * c[1] + 4 * P], bank, ACT.Copy).then_inc(hi_ok, 1)
                elif c[0] == "exp":
                    g = c[1]
                    if g >= 2:
                        act.wait_ge(scores_ok, g - 1)
                    for j in range(TG):
                        t = TG * g + j
                        act.wait_ge(shifted_ok, t + 1)
                        act.activation(expo[:, g % 2, j, :], shifted[:, g % 2, j, 0:E], ACT.Exp,
                                       accum_out=esum[:, t:t + 1]).then_inc(exp_ok, 1)
                elif c[0] == "qkv":
                    qkv_copy(c[1])

            def gxT_copy(i):
                act.wait_ge(gtr_ok, i + 1)
                if i >= 2:
                    act.wait_ge(up_ok, i - 1)
                act.activation(gxT[:, i % 2, :, :], ps[:, B_GXT, 0:D].rearrange("p (k c) -> p k c", k=KD),
                               ACT.Copy).then_inc(gxT_ok, 1)

            def silu(i):
                act.wait_ge(up_ok, i + 1)
                if i:
                    act.wait_ge(hid_ok, i)
                act.activation(sg[:, :], ps[:, B_H, 0:I], ACT.Silu).then_inc(sg_ok, 1)

            def q_high(t):
                act.wait_ge(qt_ok, t + 1)
                if t >= 2:
                    act.wait_ge(dense_ok, t - 1)
                act.activation(qT_hi[:, t % 2, :, :], ps[:, B_QT[t % 2], 0:D].rearrange("p (k c) -> p k c", k=KD),
                               ACT.Copy).then_inc(qhi_ok, 1)

            gxT_copy(0)
            qkv_copy(EARLY_T - 1)
            silu(0)
            gxT_copy(1)
            for i in range(NP):
                act.wait_ge(ht_ok, i + 1)
                if i + 2 < NP:
                    gxT_copy(i + 2)
                if i:
                    act.wait_ge(down_ok, i)
                act.activation(hidT[:, :], ps[0:I, B_GXT, D:D + P], ACT.Copy).then_inc(hidT_ok, 1)
                qts = [f[1] for f in FILL[i] if f[0] == "qt"]
                for t in qts[:1]:
                    q_high(t)
                if i + 1 < NP:
                    silu(i + 1)
                for f in FILL[i]:
                    if f[0] == "qkv":
                        qkv_copy(f[1])
                    elif f[0] == "hid":
                        g = f[1]
                        act.wait_ge(shup_ok, 3 * g + 3)
                        if g:
                            act.wait_ge(shid_ok, 2 * g)
                        act.activation(sh_sg[:, 0, :], ps[:, B_SH[0], :], ACT.Silu).then_inc(silu_ok, 1)
                        act.activation(sh_sg[0:SI - P, 1, :], ps[0:SI - P, B_SH[1], :], ACT.Silu).then_inc(silu_ok, 1)
                    elif f[0] == "split":
                        g = f[1]
                        act.wait_ge(shid_ok, 2 * g + 1)
                        if g:
                            act.wait_ge(shd_ok, 2 * g)
                        act.activation(sh_hi[:, 0, :], sh_hid[:, 0, :], ACT.Copy).then_inc(shhi_ok, 1)
                        act.wait_ge(shid_ok, 2 * g + 2)
                        act.activation(sh_hi1[0:SI - P, :], sh_hid[0:SI - P, 1, :], ACT.Copy)
                        act.activation(sh_hi[0:SI - P, 1, :], sh_hid[0:SI - P, 1, :], ACT.Copy).then_inc(shhi_ok, 1)
                for t in qts[1:]:
                    q_high(t)
            for n in range(NT // PART):
                act.wait_ge(total_ok, n + 1)
                act.dma_start(out_d[:, PART * n:PART * n + PART, :], x[:, PART * n:PART * n + PART, :]).then_inc(out_done, 16)
            act.wait_ge(out_done, 16 * NT // PART)

        def passes(hi_a, lo_a, hi_b, lo_b):
            return ((hi_a, hi_b), (hi_a, lo_b), (lo_a, hi_b))

        @block.tensor
        def _(pe):
            def project(t):
                if t == 0:
                    pe.wait_ge(wlo_ok, 3)
                    pe.wait_ge(hi_ok, number[("w", 2)] + 1)
                    pe.wait_ge(bias_ok, 1)
                if t < 2:
                    n = max(number[c] for c in before_qkv if bank_of[c] in (B_QK[t], B_V, B_A))
                    pe.wait_ge(hi_ok, n + 1)
                    pe.wait_ge(lo_ok, lows(n + 1))
                else:
                    pe.wait_ge(qkv_copied, t - 1)
                for o, cols in ((ps[:, B_QK[t % 2], :], slice(0, 2 * D)), (ps[:, B_V, 0:D], slice(2 * D, 3 * D))):
                    if t and cols.start:
                        pe.wait_ge(v_copied, t)
                    mms = [(ones[:, :], bias_hl[:, cols])]
                    mms += [(a[:, kd, P * t:P * t + P], b[:, kd, cols])
                            for kd in range(KD) for a, b in passes(xT_hi, xT_lo, wT_hi, wT_lo)]
                    for m, (a, b) in enumerate(mms):
                        mm = pe.matmul(o, a, b, start=(m == 0), stop=(m == len(mms) - 1))
                mm.then_inc(qkv_ok, 1)

            pe.wait_ge(ident_ok, 1)
            for _ in range(WARM_UP):
                pe.transpose(ps[:, B_A, 0:P], ident[:, :], ident[:, :])
            pe.wait_ge(gate_in, 16)
            for c in order:
                if c[0] in ("gate", "x", "w", "key", "sd", "wo"):
                    n = number[c]
                    bank = ps[:, bank_of[c], :]
                    if freed[c]:
                        pe.wait_ge(hi_ok, freed[c])
                        pe.wait_ge(lo_ok, lows(freed[c]))
                if c[0] == "gate":
                    for kd in range(KD):
                        tr = pe.transpose(bank[:, E * kd:E * kd + E], w_raw[0:E, 11, P * kd:P * kd + P], ident[0:E, 0:E])
                    tr.then_inc(chunk_ok, 1)
                elif c[0] == "x":
                    g, kd = c[1] // 2, c[1] % 2
                    for j, t in enumerate(tiles(g)):
                        pe.wait_ge(xn_ok, t + 1)
                        tr = pe.transpose(bank[:, P * j:P * j + P], xn[:, t, P * kd:P * kd + P], ident[:, :])
                    tr.then_inc(chunk_ok, 1)
                elif c[0] == "w":
                    pe.wait_ge(*((win_in, 16) if c[1] < 3 else (sh_in, 64)))
                    blocks = (w_cols(c[1]).stop - w_cols(c[1]).start) // P
                    for b in range(blocks):
                        for kd in range(KD):
                            src = 2 * c[1] + b if c[1] < 3 else 2 * c[1] + b + 2
                            at = P * (blocks * kd + b)
                            tr = pe.transpose(bank[:, at:at + P], w_raw[:, src, P * kd:P * kd + P], ident[:, :])
                    tr.then_inc(chunk_ok, 1)
                elif c[0] == "sd":
                    pe.wait_ge(sd_in, 16)
                    for b in range(2):
                        pe.transpose(bank[:, P * b:P * b + P], sd_raw[:, b, 0:P], ident[:, :])
                        tr = pe.transpose(bank[0:SI - P, D + P * b:D + P * b + P], sd_raw[:, b, P:SI], ident[:, :])
                    tr.then_inc(chunk_ok, 1)
                elif c[0] == "wo":
                    pe.wait_ge(wout_in, 16)
                    for kd in range(KD):
                        for b in range(2):
                            at = P * (2 * kd + b)
                            tr = pe.transpose(bank[:, at:at + P], w_raw[:, 6 + b, P * kd:P * kd + P], ident[:, :])
                    tr.then_inc(chunk_ok, 1)
                elif c[0] == "key":
                    pe.wait_ge(marked_ok, NG)
                    for j in range(4):
                        tr = pe.transpose(bank[:, P * j:P * j + P],
                                          key[:, 4 * c[1] + j, :, :].rearrange("p h e -> p (h e)"), ident[:, :])
                    tr.then_inc(chunk_ok, 1)
                elif c[0] == "logits":
                    g = c[1]
                    n = number[("x", 2 * g + 1)]
                    pe.wait_ge(hi_ok, n + 1)
                    pe.wait_ge(lo_ok, lows(n + 1))
                    if g >= 2:
                        pe.wait_ge(shifted_ok, TG * (g - 1))
                    mms = [(gateT[:, kd, :], a[:, kd, GT * g:GT * g + GT]) for kd in range(KD) for a in (xT_hi, xT_lo)]
                    for m, (a, b) in enumerate(mms):
                        mm = pe.matmul(ps[:, B_LOGITS[g % 2], :], a, b, start=(m == 0), stop=(m == len(mms) - 1))
                    mm.then_inc(lgT_ok, 1)
                elif c[0] == "tok":
                    g = c[1]
                    pe.wait_ge(sel_ok, 1)
                    pe.wait_ge(lcopy_ok, g + 1)
                    for j, t in enumerate(tiles(g)):
                        mm = pe.matmul(logits(t), lgT[:, g % 2, P * j:P * j + P], sel[:, :], start=True, stop=True)
                    mm.then_inc(logits_ok, 1)
                elif c[0] == "qkv":
                    project(c[1])
                elif c[0] == "slots":
                    pe.wait_ge(slots_ok, 1)
                    pe.transpose(ps[:, B_SLOTS, 0:E], slots[:, :, :].rearrange("e two c -> e (two c)"),
                                 ident[0:E, 0:E]).then_inc(slotsT_ok, 1)


            def gx_transposes(i):
                pe.wait_ge(gx_in[i % 4], 16 * (i // 4 + 1))
                if i:
                    pe.wait_ge(gxT_ok, i)
                if i >= 3:
                    pe.wait_ge(hidT_ok, i - 2)
                for kd in range(KD):
                    tr = pe.transpose(ps[:, B_GXT, 0:D][:, P * kd:P * kd + P], gx[:, i % 4, kd:D:KD], ident[:, :])
                tr.then_inc(gtr_ok, 1)

            def shared_up(g, b):
                if b == 0 and g == 0:
                    pe.wait_ge(qkv_copied, NT)
                elif b == 0:
                    pe.wait_ge(shid_ok, 2 * g)
                cols = slice(SH0 + P * b, SH0 + P * b + P)
                mms = [(w[:, kd, cols], xx[:, kd, GT * g:GT * g + GT])
                       for kd in range(KD) for w, xx in passes(wT_hi, wT_lo, xT_hi, xT_lo)]
                for m, (a, r) in enumerate(mms):
                    mm = pe.matmul(ps[:, B_SH[b], :], a, r, start=(m == 0), stop=(m == len(mms) - 1))
                mm.then_inc(shup_ok, 1)

            def shared_down(t2):
                g = t2 // 2
                pe.wait_ge(shhi_ok, 2 * g + 2)
                pe.wait_ge(shlo_ok, 2 * g + 2)
                if t2:
                    pe.wait_ge(shadd_ok, t2)
                else:
                    pe.wait_ge(sdb_ok, 2)
                    pe.wait_ge(wlo_ok, 6)
                    pe.wait_ge(vconst_ok, 5)
                    pe.wait_ge(acol_ok, 1)
                for half in range(2):
                    j = 2 * (t2 % 2) + half
                    mms = [(a, b) for a, b in passes(sh_hi[:, 0, P * j:P * j + P], sh_lo[:, P * j:P * j + P],
                                                     sdT_hi[:, 0, :], sdT_lo[:, 0, :])]
                    mms += [(sh_hi[:, 1, P * j:P * j + P], sdT_hi[:, 1, :]), (sh_hi1[:, P * j:P * j + P], sdT_lo[:, 1, :])]
                    for m, (a, b) in enumerate(mms):
                        mm = pe.matmul(ps[:, B_SHD, D * half:D * half + D], a, b, start=(m == 0), stop=(m == len(mms) - 1))
                mm.then_inc(shd_ok, 1)

            def q_transposes(t):
                pe.wait_ge(qrot_ok, t + 1)
                pe.wait_ge(shid_ok, 2 * NG)
                if t >= 2:
                    pe.wait_ge(qhi_ok, t - 1)
                    pe.wait_ge(qlo_ok, t - 1)
                for kd in range(KD):
                    tr = pe.transpose(ps[:, B_QT[t % 2], 0:D][:, P * kd:P * kd + P], q[:, t, P * kd:P * kd + P], ident[:, :])
                tr.then_inc(qt_ok, 1)

            def dense(t):
                pe.wait_ge(qlo_ok, t + 1)
                pe.wait_ge(woa_ok, 1 + t // SEQ_TILES)
                if t == 1:
                    pe.wait_ge(shadd_ok, NT // 2)
                if t >= 2:
                    pe.wait_ge(dadd_ok, t - 1)
                s = t // SEQ_TILES
                mms = [(a[:, t % 2, kd, :], b[:, s, kd, :])
                        for kd in range(KD) for a, b in passes(qT_hi, qT_lo, woA_hi, woA_lo)]
                for m, (a, b) in enumerate(mms):
                    mm = pe.matmul(ps[:, B_OUT[t % 2], 0:D], a, b, start=(m == 0), stop=(m == len(mms) - 1))
                mm.then_inc(dense_ok, 1)

            pe.wait_ge(hi_ok, len(chunks))
            pe.wait_ge(index_ok, 1)

            def up(i):
                pe.wait_ge(gxT_ok, i + 1)
                pe.wait_ge(gu_in[i % NW], 32 * (i // NW + 1))
                if i:
                    pe.wait_ge(hid_ok, i)
                for kd in range(KD):
                    for e in range(2):
                        mm = pe.matmul(ps[CAP * e:CAP * e + CAP, B_H, 0:2 * I], gxT[:, i % 2, kd, CAP * e:CAP * e + CAP],
                                       gu[:, i % NW, e, kd, :], start=(kd == 0), stop=(kd == KD - 1))
                mm.then_inc(up_ok, 1)

            gx_transposes(0)
            project(EARLY_T - 1)
            up(0)
            gx_transposes(1)
            for i in range(NP):
                if i + 2 < NP:
                    gx_transposes(i + 2)
                qts = [f[1] for f in FILL[i] if f[0] == "qt"]
                for t in qts[:1]:
                    q_transposes(t)
                pe.wait_ge(hid_ok, i + 1)
                pe.transpose(ps[0:I, B_GXT, D:D + P], hid[:, :], ident[:, :]).then_inc(ht_ok, 1)
                if i + 1 < NP:
                    up(i + 1)
                for f in FILL[i]:
                    if f[0] == "qkv":
                        project(f[1])
                    elif f == ("scale", 0):
                        pe.wait_ge(a_ok, NT)
                        for j in range(4):
                            mm = pe.matmul(ps[:, B_A, j:j + 1], acc[:, j // KD, P * (j % KD):P * (j % KD) + P],
                                           ones[:, 0:1].bitcast(F32), start=True, stop=True)
                        mm.then_inc(aT_ok, 1)
                    elif f[0] == "up":
                        shared_up(f[1], f[2])
                    elif f[0] == "down":
                        shared_down(f[1])
                for t in qts[1:]:
                    q_transposes(t)
                for t in qts:
                    if t:
                        dense(t - 1)
                if i == NP - 1:
                    dense(NT - 1)
                pe.wait_ge(hidT_ok, i + 1)
                pe.wait_ge(dn_in[i % NW], 16 * (i // NW + 1))
                if i >= 2:
                    pe.wait_ge(eo_ok, i - 1)
                for e in range(2):
                    mm = pe.matmul(ps[CAP * e:CAP * e + CAP, B_EO[i % 2], 0:D], hidT[:, CAP * e:CAP * e + CAP],
                                   dn[:, i % NW, e, :], start=True, stop=True)
                mm.then_inc(down_ok, 1)

        @block.vector
        def _(dve):
            steps = [0]

            def step(ins):
                steps[0] += 1
                ins.then_inc(vstep, 1)
                return steps[0]

            def done(ins):
                dve.wait_ge(vstep, step(ins))

            def layer_stats(g):
                dve.wait_ge(x_in[g], 16)
                for t in tiles(g):
                    n = step(dve.bn_stats(stats[:, t, :], x[:, t, :]))
                dve.wait_ge(vstep, n)
                for t in tiles(g):
                    n = step(dve.bn_aggr(mv[:, t, :], stats[:, t, :]))
                dve.wait_ge(vstep, n)
                dve.tensor_scalar(var[:, TG * g:TG * g + TG], mv[:, TG * g:TG * g + TG, 1], EPS, None,
                                  ALU.add).then_inc(var_ok, 1)

            def minus_mean(g):
                s = slice(TG * g, TG * g + TG)
                dve.wait_ge(rstd_ok, g + 1)
                dve.scalar_tensor_tensor(out=nmr[:, s], in0=mv[:, s, 0], scalar=-1.0, in1=rstd[:, s],
                                         op0=ALU.mult, op1=ALU.mult).then_inc(nmr_ok, 1)

            def normalise(g):
                dve.wait_ge(rstd_ok, g + 1)
                dve.wait_ge(xn_ok, TG * g)
                for t in tiles(g):
                    dve.tensor_scalar(xn[:, t, :], x[:, t, :], mv[:, t, 0:1], rstd[:, t:t + 1],
                                      ALU.subtract, ALU.mult).then_inc(xn_ok, 1)

            def low_part(c):
                n = number[c]
                bank = ps[:, bank_of[c], :]
                dve.wait_ge(hi_ok, n + 1)
                if c[0] == "gate":
                    dve.tensor_tensor(gateT[:, :, E:2 * E], bank[:, 0:KD * E].rearrange("p (k e) -> p k e", k=KD),
                                      gateT[:, :, 0:E].bitcast(F32), ALU.subtract).then_inc(lo_ok, 1)
                else:
                    g, kd = c[1] // 2, c[1] % 2
                    s = slice(GT * g, GT * g + GT)
                    dve.tensor_tensor(xT_lo[:, kd, s], bank, xT_hi[:, kd, s].bitcast(F32), ALU.subtract).then_inc(lo_ok, 1)

            def choose(g):
                dve.wait_ge(logits_ok, g + 1)
                for t in tiles(g):
                    n = step(dve.max(best[:, t, :], logits(t)))
                dve.wait_ge(vstep, n)
                if g >= 2:
                    dve.wait_ge(exp_ok, TG * (g - 1))
                for j, t in enumerate(tiles(g)):
                    dve.tensor_scalar(shifted[:, g % 2, j, 0:E], logits(t), best[:, t, 0:1], LOWEST,
                                      ALU.subtract, ALU.max).then_inc(shifted_ok, 1)
                s = slice(TG * g, TG * g + TG)
                done(dve.tensor_tensor(best_sh[:, :, 0:TOPK], best[:, s, 0:TOPK],
                                       best[:, s, 0:1].to_broadcast([P, TG, TOPK]), ALU.subtract))
                done(dve.tensor_scalar(best_sh[:, :, 0:TOPK], best_sh[:, :, 0:TOPK], LOWEST, None, ALU.max))
                dve.wait_ge(shifted_ok, TG * g + TG)
                for j in range(TG):
                    n = step(dve.match_replace(marked[:, j, :], best_sh[:, j, :], shifted[:, g % 2, j, :], CHOSEN))
                dve.wait_ge(vstep, n)
                j0 = TG * g % SEQ_TILES
                dve.scalar_tensor_tensor(out=key[:, j0:j0 + TG, g // 2, :], in0=marked[:, :, 0:E], scalar=CHOSEN,
                                         in1=kconst[:, s].unsqueeze(2).to_broadcast([P, TG, E]),
                                         op0=ALU.is_equal, op1=ALU.mult).then_inc(marked_ok, 1)

            def invert_sums(g):
                s = slice(TG * g, TG * g + TG)
                dve.wait_ge(exp_ok, TG * g + TG)
                dve.reciprocal(einv[:, s], esum[:, s]).then_inc(einv_ok, 1)

            dve.memset(zeros[:, :], 0.0).then_inc(vconst_ok, 1)
            dve.wait_ge(ident_ok, 1)
            dve.tensor_tensor(sel[:, :], ident[:, 0:E], ident[:, E:2 * E], ALU.add).then_inc(sel_ok, 1)
            dve.memset(bias[0:33, :], 0.0).then_inc(vconst_ok, 1)
            n = step(dve.memset(shifted[:, :, :, E:E + 2], PADDED))
            n = step(dve.memset(best_sh[:, :, TOPK:8], PADDED))
            dve.memset(bias_hl[:, :].bitcast(F32), 0.0).then_inc(vconst_ok, 1)
            n = step(dve.memset(ones[:, :].bitcast(F32), 1.0))
            dve.memset(sdT_lo[SI - P:P, 1, :].bitcast(F32), 0.0).then_inc(vconst_ok, 1)
            dve.memset(sh_hi1[SI - P:P, :].bitcast(F32), 1.0).then_inc(vconst_ok, 1)
            dve.wait_ge(iota_ok, 1)
            n = step(dve.tensor_copy(kconst[:, :], kconst_i[:, :]))
            n = step(dve.tensor_copy(cpart[:, :], cpart_i[:, :]))
            dve.wait_ge(vstep, n)

            layer_stats(0)
            layer_stats(1)
            minus_mean(0)
            layer_stats(2)
            minus_mean(1)
            low_part(("gate", 0))
            low_part(("x", 0))
            low_part(("x", 1))
            layer_stats(3)
            minus_mean(2)
            low_part(("x", 2))
            low_part(("x", 3))
            normalise(3)
            choose(0)
            low_part(("x", 4))
            low_part(("x", 5))
            invert_sums(0)
            choose(1)
            low_part(("x", 6))
            low_part(("x", 7))
            choose(2)
            invert_sums(1)
            choose(3)
            invert_sums(2)

            dve.wait_ge(hi_ok, number[("key", 1)] + 1)
            for r in range(CAP // 8):
                done(dve.max(cand[:, 8 * r:8 * r + 8], keyT[:, :]))
                if r + 1 < CAP // 8:
                    done(dve.match_replace(keyT[:, :], cand[:, 8 * r:8 * r + 8], keyT[:, :], -1.0))
                if r == 0:
                    invert_sums(3)
            done(dve.tensor_copy(other[:, :], cand[E:2 * E, ::-1]))
            for copy in range(2):
                n = step(dve.tensor_tensor(slots[:, copy, :], cand[0:E, :], other[:, :], ALU.max))
            dve.wait_ge(vstep, n)
            dve.sem_inc(slots_ok, 1)

            dve.wait_ge(slotsT_ok, 1)
            slotsT = ps[:, B_SLOTS, 0:E].rearrange("c (i two) -> c i two", two=2)
            n = step(dve.tensor_copy(keyc[0:CAP, :], slotsT[0:CAP, :, 0]))
            done(dve.tensor_copy(keyc[CAP:P, :], slotsT[CAP:P, :, 1]))
            n = step(dve.tensor_scalar(tokf[:, :], keyc[:, :], -1.0, float(T), ALU.mult, ALU.add))
            done(dve.tensor_scalar(padc[:, :], keyc[:, :], 0.0, cpart[:, :], ALU.is_equal, ALU.mult))
            n = step(dve.scalar_tensor_tensor(out=to_row[:, NP - 1:NP], in0=padc[:, NP - 1:NP], scalar=base_last[:, :],
                                              in1=keyc[:, NP - 1:NP], op0=ALU.add, op1=ALU.subtract))
            n = step(dve.tensor_scalar(from_row[:, :], tokf[:, :], float(T - 1), None, ALU.min))
            done(dve.scalar_tensor_tensor(out=to_row[:, 0:NP - 1], in0=padc[:, 0:NP - 1], scalar=base[:, :], in1=keyc[:, 0:NP - 1],
                                          op0=ALU.add, op1=ALU.subtract))
            done(dve.tensor_copy(to_last[:, :], to_row[CAP:P, NP - 1:NP]))
            dve.sem_inc(index_ok, 1)

            def scale_wout(s):
                if s == 0:
                    dve.wait_ge(aT_ok, 1)
                    dve.wait_ge(hi_ok, number[("wo", 0)] + 1)
                    dve.tensor_copy(acol[:, :], ps[:, B_A, 0:4]).then_inc(acol_ok, 1)
                    dve.wait_ge(acol_ok, 1)
                for kd in range(KD):
                    a = acol[:, 2 * s + kd:2 * s + kd + 1]
                    n = step(dve.tensor_scalar(woA[:, s, kd, :], woT[:, kd, :], a, None, ALU.mult))
                dve.wait_ge(vstep, n)
                done(dve.tensor_copy(woA_hi[:, s, :, :], woA[:, s, :, :]))
                dve.tensor_tensor(woA_lo[:, s, :, :], woA[:, s, :, :], woA_hi[:, s, :, :].bitcast(F32),
                                  ALU.subtract).then_inc(woa_ok, 1)

            dve.wait_ge(table_in, 32)
            dve.wait_ge(kv_ok, POOL_T)

            def accumulate(t):
                s = t // SEQ_TILES
                dve.wait_ge(kv_ok, t + 1)
                dve.wait_ge(rnorm_ok, t + 1)
                if t:
                    dve.wait_ge(a_ok, t)
                if t % SEQ_TILES == 0:
                    dve.tensor_scalar(acc[:, s, :], kv[:, t % POOL_T, :], rnorm[:, t:t + 1], None, ALU.mult).then_inc(a_ok, 1)
                else:
                    dve.scalar_tensor_tensor(out=acc[:, s, :], in0=kv[:, t % POOL_T, :], scalar=rnorm[:, t:t + 1],
                                             in1=acc[:, s, :], op0=ALU.mult, op1=ALU.add).then_inc(a_ok, 1)

            for t in range(POOL_T, EARLY_T - 1):
                accumulate(t - POOL_T)
                rotate_k(dve, done, t)

            def take_scores(i):
                dve.wait_ge(gx_in[i % 4], 16 * (i // 4 + 1))
                if i >= 4:
                    dve.wait_ge(hid_ok, i - 3)
                for e in range(2):
                    s = slice(CAP * e, CAP * e + CAP)
                    dve.tensor_copy(wsl[s, i % 4:i % 4 + 1], gx[s, i % 4, D + 2 * i + e:D + 2 * i + e + 1]).then_inc(wsl_ok, 1)

            def hidden(i):
                dve.wait_ge(sg_ok, i + 1)
                dve.wait_ge(wsl_ok, 2 * i + 2)
                if i:
                    dve.wait_ge(ht_ok, i)
                dve.scalar_tensor_tensor(out=hid[:, :], in0=sg[:, :], scalar=wsl[:, i % 4:i % 4 + 1],
                                         in1=ps[:, B_H, I:2 * I], op0=ALU.mult, op1=ALU.mult).then_inc(hid_ok, 1)

            def output(i):
                dve.wait_ge(down_ok, i + 1)
                if i >= 4:
                    dve.wait_ge(scattered, 16 * (i - 3))
                dve.tensor_copy(eo[:, i % 4, :], ps[:, B_EO[i % 2], 0:D]).then_inc(eo_ok, 1)

            def q_low(t):
                dve.wait_ge(qhi_ok, t + 1)
                if t >= 2:
                    dve.wait_ge(dense_ok, t - 1)
                dve.tensor_tensor(qT_lo[:, t % 2, :, :], ps[:, B_QT[t % 2], 0:D].rearrange("p (k c) -> p k c", k=KD),
                                  qT_hi[:, t % 2, :, :].bitcast(F32), ALU.subtract).then_inc(qlo_ok, 1)

            def add_dense(t):
                dve.wait_ge(dense_ok, t + 1)
                dve.wait_ge(shadd_ok, NT // 2)
                dve.tensor_tensor(x[:, t, :], ps[:, B_OUT[t % 2], 0:D], x[:, t, :], ALU.add).then_inc(dadd_ok, 1)

            take_scores(0)
            take_scores(1)
            hidden(0)
            accumulate(EARLY_T - 1 - POOL_T)
            rotate_k(dve, done, EARLY_T - 1)
            for i in range(NP):
                if i:
                    output(i - 1)
                if i < 3:
                    left = range(EARLY_T - POOL_T, EARLY_T)
                    for t in left[len(left) * i // 3:len(left) * (i + 1) // 3]:
                        accumulate(t)
                for f in FILL[i - 2] if i >= 2 else []:
                    if f[0] == "qkv":
                        accumulate(f[1])
                for f in FILL[i - 1] if i else []:
                    if f[0] == "qkv":
                        rotate_k(dve, done, f[1])
                    elif f[0] == "down":
                        t2 = f[1]
                        xx = x[:, 2 * t2:2 * t2 + 2, :]
                        dve.wait_ge(shd_ok, t2 + 1)
                        dve.wait_ge(resid_ok, NG)
                        dve.tensor_tensor(xx, ps[:, B_SHD, :].rearrange("p (n d) -> p n d", n=2), xx,
                                          ALU.add).then_inc(shadd_ok, 1)
                if i + 2 < NP:
                    take_scores(i + 2)
                qts = [f[1] for f in FILL[i] if f[0] == "qt"]
                for t in qts[:1]:
                    if t >= 2:
                        add_dense(t - 2)
                    q_low(t)
                if i + 1 < NP:
                    hidden(i + 1)
                for f in FILL[i]:
                    if f[0] == "scale":
                        scale_wout(f[1])
                    elif f[0] == "rotq":
                        t = f[1]
                        dve.wait_ge(qkv_copied, t + 1)
                        if t:
                            dve.wait_ge(qrot_ok, t)
                        rotate(dve, done, q[:, t, :], rot_q, *tables(t)).then_inc(qrot_ok, 1)
                    elif f[0] == "hid":
                        g = f[1]
                        dve.wait_ge(silu_ok, 2 * g + 1)
                        if g:
                            dve.wait_ge(shhi_ok, 2 * g)
                            dve.wait_ge(shlo_ok, 2 * g)
                        dve.tensor_tensor(sh_hid[:, 0, :], sh_sg[:, 0, :], ps[:, B_SH[2], :], ALU.mult).then_inc(shid_ok, 1)
                        dve.wait_ge(silu_ok, 2 * g + 2)
                        dve.tensor_tensor(sh_hid[0:SI - P, 1, :], sh_sg[0:SI - P, 1, :], ps[SI - P:P, B_SH[1], :],
                                          ALU.mult).then_inc(shid_ok, 1)
                    elif f[0] == "split":
                        g = f[1]
                        dve.wait_ge(shhi_ok, 2 * g + 1)
                        if g:
                            dve.wait_ge(shd_ok, 2 * g)
                        dve.tensor_tensor(sh_lo[:, :], sh_hid[:, 0, :], sh_hi[:, 0, :].bitcast(F32),
                                          ALU.subtract).then_inc(shlo_ok, 1)
                        dve.wait_ge(shhi_ok, 2 * g + 2)
                        dve.tensor_tensor(sh_hi[SI - P:P, 1, :], sh_hid[0:SI - P, 1, :],
                                          sh_hi[0:SI - P, 1, :].bitcast(F32), ALU.subtract).then_inc(shlo_ok, 1)
                for t in qts[1:]:
                    q_low(t)
                    if t >= 2:
                        add_dense(t - 2)
            add_dense(NT - 2)
            output(NP - 1)
            add_dense(NT - 1)

            dve.wait_ge(dadd_ok, NT)
            for n in range(NT // PART):
                s = slice(PART * n, PART * n + PART)
                dve.wait_ge(sum_in[n], 16)
                dve.tensor_tensor(x[:, s, :], x[:, s, :], q[:, s, :], ALU.add).then_inc(half_sum, 1)
            for n in range(NT // PART):
                s = slice(PART * n, PART * n + PART)
                dve.wait_ge(half_sum, n + 1)
                dve.wait_ge(sum1_in[n], 16)
                dve.tensor_tensor(x[:, s, :], x[:, s, :], w_raw[:, PART * (n % RING):PART * (n % RING) + PART, :],
                                  ALU.add).then_inc(total_ok, 1)


_INS = ['L0_attn_X', 'L0_attn_W_in', 'L0_attn_b_in', 'L0_attn_W_out', 'L0_attn_b_out', 'L0_ffn_gate_w',
        'L0_ffn_gate_up_proj', 'L0_ffn_down_proj', 'L0_ffn_shared_gate_w', 'L0_ffn_shared_up_w',
        'L0_ffn_shared_down_w']
_OUTS = [((2, 1024, 256), 'float32')]


def rope_tables(seq, rot):
    import numpy as _np
    inv = (1.0 / _np.float32(10000.0) ** (_np.arange(0, rot, 2, dtype=_np.float32) / _np.float32(rot))).astype(_np.float32)
    angle = _np.repeat(_np.arange(seq, dtype=_np.float32)[:, None] * inv[None, :], 2, axis=-1)
    sign = _np.where(_np.arange(rot) % 2 == 0, _np.float32(-1), _np.float32(1))
    return _np.cos(angle).astype(_np.float32), (_np.sin(angle) * sign).astype(_np.float32)


def kernel(**inputs):
    import numpy as _np
    import concourse.bacc as _bacc
    from concourse import mybir as _mybir
    from concourse.bass_utils import run_bass_kernel_spmd as _run

    nc = _bacc.Bacc("TRN2", target_bir_lowering=False, num_devices=1)
    arrays, args = {}, []
    named = [(name, _np.ascontiguousarray(inputs[name])) for name in _INS]
    named += list(zip(("cos_table", "sin_table"), rope_tables(1024, 128)))
    for name, a in named:
        arrays[f"in_{name}_dram"] = a
        args.append(nc.dram_tensor(f"in_{name}_dram", a.shape, _mybir.dt.from_np(a.dtype), kind="ExternalInput").ap())
    for i, (shape, dtype) in enumerate(_OUTS):
        dt = _mybir.dt.from_np(_np.dtype(dtype))
        args.append(nc.dram_tensor(f"out_{i}_dram", shape, dt, kind="ExternalOutput").ap())
    rows = nc.dram_tensor("token_rows", (T, ROW), _mybir.dt.float32, kind="Internal").ap()
    sums = nc.dram_tensor("expert_sums", (2 * SUMROWS, D), _mybir.dt.float32, kind="Internal").ap()
    build(nc, *args, rows, sums)
    r = _run(nc, [arrays], core_ids=[0])
    return r.results[0]["out_0_dram"]
```
